# Optimizing a Trainium2 kernel written in Bass

```python
import numpy as np
import jax
import jax.numpy as jnp

def _softmax(x, axis=-1):
    return jax.nn.softmax(x, axis=axis)

def _gelu(x):
    return jax.nn.gelu(x, approximate=True)

def _silu(x):
    return jax.nn.silu(x)

def _sigmoid(x):
    return jax.nn.sigmoid(x)

def _layernorm(x, axis=-1, eps=1e-05):
    m = jnp.mean(x, axis=axis, keepdims=True)
    v = jnp.var(x, axis=axis, keepdims=True)
    return (x - m) / jnp.sqrt(v + eps)

def _scatter_add(tgt, idx, src, axis=0):
    return tgt.at[idx].add(src)

def _segment_sum(src, seg, n):
    return jax.ops.segment_sum(src, seg, n)
kernel_name = 'mk_metaformer_d1_conv_nchw256_r4_a75307'

def setup_inputs(seed: int=0):
    np.random.seed(seed)
    _w = jnp.asarray

    def _rec_inputs():
        import jax
        import jax.numpy as jnp
        _gk = jax.random.key(seed)
        x = -0.0002091 + 1 * jax.random.normal(jax.random.fold_in(_gk, 1), (32, 64, 56, 56), jnp.float32)
        return x
    x = _rec_inputs()

    def _L0_conv_setup():
        import jax, jax.numpy as jnp
        import numpy as np
        K = 10.0
        T = 0.1
        BN_EPS = 1e-05

        @jax.custom_vjp
        def binary_quantize(x):
            return jnp.sign(x)

        def _bq_fwd(x):
            return (jnp.sign(x), x)

        def _bq_bwd(x, g):
            return (K * T * (1.0 - jnp.tanh(x * T) ** 2) * g,)
        binary_quantize.defvjp(_bq_fwd, _bq_bwd)

        def _convalg(x, weight, gamma, beta):
            co = weight.shape[0]
            wf = weight.reshape(co, -1)
            bw = weight - wf.mean(-1).reshape(co, 1, 1, 1)
            std = jnp.std(bw.reshape(co, -1), axis=-1, ddof=1).reshape(co, 1, 1, 1)
            bw = bw / std
            sw = jax.lax.stop_gradient(2.0 ** jnp.round(jnp.log2(jnp.abs(bw).reshape(co, -1).mean(-1)))).reshape(co, 1, 1, 1)
            bwq = binary_quantize(bw) * sw
            ba = binary_quantize(x)
            y = jax.lax.conv_general_dilated(ba, bwq, window_strides=(1, 1), padding=((1, 1), (1, 1)), dimension_numbers=('NCHW', 'OIHW', 'NCHW'))
            mean = y.mean(axis=(0, 2, 3), keepdims=True)
            var = y.var(axis=(0, 2, 3), keepdims=True)
            yn = (y - mean) * jax.lax.rsqrt(var + BN_EPS)
            yn = yn * gamma.reshape(1, -1, 1, 1) + beta.reshape(1, -1, 1, 1)
            return jnp.clip(yn, -1.0, 1.0)
        key = jax.random.key(seed)
        k1, k2 = jax.random.split(key, 2)
        return {'x': jax.random.normal(k1, (32, 64, 56, 56), dtype=jnp.float32), 'weight': jax.random.normal(k2, (64, 64, 3, 3), dtype=jnp.float32) * 0.05, 'gamma': jnp.ones((64,), dtype=jnp.float32), 'beta': jnp.zeros((64,), dtype=jnp.float32)}
    _L0_conv_all = _L0_conv_setup()
    _L0_conv_in = {k: v for k, v in _L0_conv_all.items() if k in ('weight', 'gamma', 'beta')}
    del _L0_conv_all

    def _L0_ffn_setup():
        import jax, jax.numpy as jnp
        import numpy as np
        BN_EPS = 0.001

        def _bn(h, g, b, m, v):
            return g * (h - m) * jax.lax.rsqrt(v + BN_EPS) + b
        key = jax.random.key(seed)
        ks = jax.random.split(key, 8)
        B, F, Df = (64, 16, 64)
        E, H, D = (8, 64, 64)
        s1 = 1.0 / np.sqrt(Df)
        s2 = 1.0 / np.sqrt(H)
        return {'x': jax.random.normal(ks[0], (B, F, Df), jnp.float32), 'Wr': jax.random.normal(ks[1], (Df, E), jnp.float32) * s1, 'br': jnp.zeros((E,), jnp.float32), 'W1': jax.random.normal(ks[2], (E, Df, H), jnp.float32) * s1, 'b1': jnp.zeros((E, H), jnp.float32), 'g1': jnp.ones((E, H), jnp.float32), 'be1': jnp.zeros((E, H), jnp.float32), 'm1': jnp.zeros((E, H), jnp.float32), 'v1': jnp.ones((E, H), jnp.float32), 'W2': jax.random.normal(ks[3], (E, H, H), jnp.float32) * s2, 'b2': jnp.zeros((E, H), jnp.float32), 'g2': jnp.ones((E, H), jnp.float32), 'be2': jnp.zeros((E, H), jnp.float32), 'm2': jnp.zeros((E, H), jnp.float32), 'v2': jnp.ones((E, H), jnp.float32), 'Wo': jax.random.normal(ks[4], (E, H, D), jnp.float32) * s2, 'bo': jnp.zeros((E, D), jnp.float32)}
    _L0_ffn_all = _L0_ffn_setup()
    _L0_ffn_in = {k: v for k, v in _L0_ffn_all.items() if k in ('Wr', 'br', 'W1', 'b1', 'g1', 'be1', 'm1', 'v1', 'W2', 'b2', 'g2', 'be2', 'm2', 'v2', 'Wo', 'bo')}
    del _L0_ffn_all
    return {'x': x, 'L0_conv_weight': _L0_conv_in['weight'], 'L0_conv_gamma': _L0_conv_in['gamma'], 'L0_conv_beta': _L0_conv_in['beta'], 'L0_ffn_Wr': _L0_ffn_in['Wr'], 'L0_ffn_br': _L0_ffn_in['br'], 'L0_ffn_W1': _L0_ffn_in['W1'], 'L0_ffn_b1': _L0_ffn_in['b1'], 'L0_ffn_g1': _L0_ffn_in['g1'], 'L0_ffn_be1': _L0_ffn_in['be1'], 'L0_ffn_m1': _L0_ffn_in['m1'], 'L0_ffn_v1': _L0_ffn_in['v1'], 'L0_ffn_W2': _L0_ffn_in['W2'], 'L0_ffn_b2': _L0_ffn_in['b2'], 'L0_ffn_g2': _L0_ffn_in['g2'], 'L0_ffn_be2': _L0_ffn_in['be2'], 'L0_ffn_m2': _L0_ffn_in['m2'], 'L0_ffn_v2': _L0_ffn_in['v2'], 'L0_ffn_Wo': _L0_ffn_in['Wo'], 'L0_ffn_bo': _L0_ffn_in['bo']}

def reference(x, L0_conv_weight, L0_conv_gamma, L0_conv_beta, L0_ffn_Wr, L0_ffn_br, L0_ffn_W1, L0_ffn_b1, L0_ffn_g1, L0_ffn_be1, L0_ffn_m1, L0_ffn_v1, L0_ffn_W2, L0_ffn_b2, L0_ffn_g2, L0_ffn_be2, L0_ffn_m2, L0_ffn_v2, L0_ffn_Wo, L0_ffn_bo):
    import jax
    import jax.numpy as jnp

    def _L0_conv_ref(x, weight, gamma, beta):
        import jax, jax.numpy as jnp
        import numpy as np
        K = 10.0
        T = 0.1
        BN_EPS = 1e-05

        @jax.custom_vjp
        def binary_quantize(x):
            return jnp.sign(x)

        def _bq_fwd(x):
            return (jnp.sign(x), x)

        def _bq_bwd(x, g):
            return (K * T * (1.0 - jnp.tanh(x * T) ** 2) * g,)
        binary_quantize.defvjp(_bq_fwd, _bq_bwd)

        def _convalg(x, weight, gamma, beta):
            co = weight.shape[0]
            wf = weight.reshape(co, -1)
            bw = weight - wf.mean(-1).reshape(co, 1, 1, 1)
            std = jnp.std(bw.reshape(co, -1), axis=-1, ddof=1).reshape(co, 1, 1, 1)
            bw = bw / std
            sw = jax.lax.stop_gradient(2.0 ** jnp.round(jnp.log2(jnp.abs(bw).reshape(co, -1).mean(-1)))).reshape(co, 1, 1, 1)
            bwq = binary_quantize(bw) * sw
            ba = binary_quantize(x)
            y = jax.lax.conv_general_dilated(ba, bwq, window_strides=(1, 1), padding=((1, 1), (1, 1)), dimension_numbers=('NCHW', 'OIHW', 'NCHW'))
            mean = y.mean(axis=(0, 2, 3), keepdims=True)
            var = y.var(axis=(0, 2, 3), keepdims=True)
            yn = (y - mean) * jax.lax.rsqrt(var + BN_EPS)
            yn = yn * gamma.reshape(1, -1, 1, 1) + beta.reshape(1, -1, 1, 1)
            return jnp.clip(yn, -1.0, 1.0)
        return _convalg(x, weight, gamma, beta)

    def _L0_ffn_ref(x, Wr, br, W1, b1, g1, be1, m1, v1, W2, b2, g2, be2, m2, v2, Wo, bo):
        import jax, jax.numpy as jnp
        import numpy as np
        BN_EPS = 0.001

        def _bn(h, g, b, m, v):
            return g * (h - m) * jax.lax.rsqrt(v + BN_EPS) + b
        feat = jnp.mean(x, axis=0)
        w = jax.nn.softmax(feat @ Wr + br, axis=-1)
        h = jnp.einsum('bfd,edh->bfeh', x, W1) + b1
        h = jax.nn.relu(_bn(h, g1, be1, m1, v1))
        h = jnp.einsum('bfeh,ehk->bfek', h, W2) + b2
        h = jax.nn.relu(_bn(h, g2, be2, m2, v2))
        y = jnp.einsum('bfeh,ehd->bfed', h, Wo) + bo
        return jnp.einsum('bfed,fe->bfd', y, w)

    def _gn(v, G=32, eps=1e-05):
        B_, C_, H_, W_ = v.shape
        g = v.reshape(B_, G, C_ // G, H_, W_)
        m = jnp.mean(g, axis=(2, 3, 4), keepdims=True)
        s = jnp.var(g, axis=(2, 3, 4), keepdims=True)
        return ((g - m) / jnp.sqrt(s + eps)).reshape(v.shape)

    def _ln_c(v, eps=1e-06):
        m = jnp.mean(v, axis=1, keepdims=True)
        s = jnp.var(v, axis=1, keepdims=True)
        return (v - m) / jnp.sqrt(s + eps)

    def _ln_t(v, eps=1e-05):
        m = jnp.mean(v, axis=-1, keepdims=True)
        s = jnp.var(v, axis=-1, keepdims=True)
        return (v - m) / jnp.sqrt(s + eps)

    def _to_tokens(v):
        B_, C_, H_, W_ = v.shape
        return v.reshape(B_, C_, H_ * W_).transpose(0, 2, 1)

    def _from_tokens(t, like):
        B_, C_, H_, W_ = like.shape
        return t.transpose(0, 2, 1).reshape(B_, C_, H_, W_)
    x = x + _L0_conv_ref(_ln_c(x), L0_conv_weight, L0_conv_gamma, L0_conv_beta)
    t = _to_tokens(x)
    t = t + _L0_ffn_ref(_ln_t(t), L0_ffn_Wr, L0_ffn_br, L0_ffn_W1, L0_ffn_b1, L0_ffn_g1, L0_ffn_be1, L0_ffn_m1, L0_ffn_v1, L0_ffn_W2, L0_ffn_b2, L0_ffn_g2, L0_ffn_be2, L0_ffn_m2, L0_ffn_v2, L0_ffn_Wo, L0_ffn_bo)
    x = _from_tokens(t, x)
    return x

_drawn_inputs = setup_inputs


def setup_inputs(seed=0):
    import zlib

    import numpy as np

    out = dict(_drawn_inputs(seed))
    spreads = {'L0_conv_gamma': (1.0, 0.2),
     'L0_conv_beta': (0.0, 0.1),
     'L0_ffn_br': (0.0, 0.329),
     'L0_ffn_b1': (0.0, 0.52),
     'L0_ffn_g1': (1.0, 0.2),
     'L0_ffn_be1': (0.0, 0.501),
     'L0_ffn_m1': (0.0, 0.542),
     'L0_ffn_v1': (1.0, 0.6),
     'L0_ffn_b2': (0.0, 0.38),
     'L0_ffn_g2': (1.0, 0.2),
     'L0_ffn_be2': (0.0, 0.42),
     'L0_ffn_m2': (0.0, 0.359),
     'L0_ffn_v2': (1.0, 0.6),
     'L0_ffn_bo': (0.0, 0.1)}
    factors = {}
    for name, (base, spread) in spreads.items():
        noise = np.random.default_rng([zlib.crc32(name.encode()), seed]).standard_normal(out[name].shape)
        drawn = base * np.exp(spread * noise) if base else spread * noise
        out[name] = jnp.asarray(drawn.astype(out[name].dtype))
    for name, factor in factors.items():
        out[name] = (out[name] * factor).astype(out[name].dtype)
    return out
```

```python
from contextlib import ExitStack

import concourse.bass as bass
from concourse import mybir

F32 = mybir.dt.float32
F32R = mybir.dt.float32r
F16 = mybir.dt.float16
BF16 = mybir.dt.bfloat16
I32 = mybir.dt.int32
ALU = mybir.AluOpType
ACT = mybir.ActivationFunctionType
AX = mybir.AxisListType

P = 128
B, C, H, W = 32, 64, 56, 56
E = 8
PAIRS = E // 2
RP = H // 2
SLOTS = RP + 1
TAPS = 9
GA = 4
KG = RP // GA
XRING = 4
G = 4
BG = B // G
NG = BG * W
UNITS = G * PAIRS
LN_EPS, BN1_EPS, BNF_EPS = 1e-5, 1e-5, 1e-3
SHIFT = 0.125
EXP_MASK = 0x7F800000
SQRT2 = 2.0 ** 0.5


def slot_group(i):
    return (0 if i == 0 else KG * i + 1), KG * (i + 1) + 1


def metaformer_kernel(nc, x, cw, gamma, beta, Wr, br, W1, b1, g1, be1, m1, v1, W2, b2, g2, be2, m2, v2, Wo, bo, out):
    with ExitStack() as ctx:
        def sb(name, shape, dt, to=ctx):
            return to.enter_context(nc.sbuf_tensor(name, shape, dt))

        def sem(name):
            return ctx.enter_context(nc.semaphore(name))

        y = sb("y", [P, RP, B, W], F16)
        ident = sb("ident", [P, P], F32)
        ones64 = sb("ones64", [P, P], F32)
        centre = sb("centre", [P, P], F32R)
        halves = sb("halves", [P, P], F32)
        convw = sb("convw", [P, 3, 2, P], BF16)
        w1hi = sb("w1hi", [P, E * C], F32R)
        w1lo = sb("w1lo", [P, E * C], F32R)
        w2hi = sb("w2hi", [P, PAIRS, P], F32R)
        w2lo = sb("w2lo", [P, PAIRS, P], F32R)
        wo = sb("wo", [P, PAIRS, C], F32)
        wr = sb("wr", [P, 2, E], F32)
        brb = sb("brb", [W, 2, E], F32)
        bias2 = sb("bias2", [P, PAIRS], F32)
        negb2 = sb("negb2", [P, PAIRS], F32)
        expert_const = sb("expert_const", [2 * E, P], F32)
        bn = sb("bn", [P, 16], F32)
        SCALE, OFFSET, SW = bn[:, 0:1], bn[:, 1:2], bn[:, 2:3]
        gb = sb("gb", [P, 2], F32)

        early = ExitStack()
        xa = sb("xa", [P, XRING, SLOTS, W], F32, early)
        xhi = sb("xhi", [P, 2, SLOTS, W], F32R, early)
        xlo = sb("xlo", [P, 2, SLOTS, W], F32R, early)
        sgn = sb("sgn", [P, 2, SLOTS, W + 2], BF16, early)
        stats = sb("stats", [P, B, GA, 6], F32, early)
        cwt = sb("cwt", [P, C, 3, 3], F32, early)
        cwa = sb("cwa", [P, C * TAPS], F32, early)
        cwsign = sb("cwsign", [C, 3, 5, C], BF16, early)
        identb = sb("identb", [C, C], BF16, early)
        rows = sb("rows", [P, 7, E * C], F32, early)
        cols = sb("cols", [P, 6, PAIRS], F32, early)
        wraw = sb("wraw", [P, E, C], F32, early)
        w2raw = sb("w2raw", [P, PAIRS, P], F32, early)
        c2sel = sb("c2sel", [P, PAIRS, 2 * E], F32, early)
        tmp = sb("tmp", [P, E * C], F32, early)
        early.close()

        late = ExitStack()
        xin = sb("xin", [P, B, W], F32, late)
        o = sb("o", [P, 2, B, W], F32, late)
        t = sb("t", [P, 2, NG], F32, late)
        ph = sb("ph", [P, 2, NG], F32R, late)
        pl = sb("pl", [P, 2, NG], F32R, late)
        xc = sb("xc", [P, 2, NG], F32, late)
        rstd = sb("rstd", [P, 2, NG], F32, late)
        u = sb("u", [P, 2, NG], F32, late)
        feat4 = sb("feat4", [P, G, W], F32, late)
        feat = sb("feat", [P, W], F32, late)
        stack = sb("stack", [P, 2, 2, G, NG], F32R, late)
        gate = sb("gate", [W, 2, E], F32, late)
        gate_e = sb("gate_e", [W, 2, E], F32, late)
        gate_w = sb("gate_w", [P, 2, E], F32, late)
        gate_s = sb("gate_s", [W, 2, 2], F32, late)
        wT = sb("wT", [2 * E, W], F32, late)
        wb = sb("wb", [P, 2, PAIRS, 2, W], F32, late)
        gconst = sb("gconst", [P, 2, W], F32, late)
        hhi = sb("hhi", [P, 2, 2, NG], F32R, late)
        hlo = sb("hlo", [P, 2, 2, NG], F32R, late)
        v = sb("v", [P, 2, 2, NG], F32, late)

        ps = ctx.enter_context(nc.psum_tensor("ps", [P, 8, 512], F32))
        misc = ps[:, 7]

        s_cw = sem("s_cw")
        s_ffn = sem("s_ffn")
        s_w2 = sem("s_w2")
        s_const = sem("s_const")
        s_zero = sem("s_zero")
        s_dve = sem("s_dve")
        s_act = sem("s_act")
        s_pe = sem("s_pe")
        s_xa = [sem(f"s_xa{i}") for i in range(XRING)]
        a_hi = sem("a_hi")
        a_split = sem("a_split")
        a_centred = sem("a_centred")
        a_signed = sem("a_signed")
        a_conv = sem("a_conv")
        a_kept = sem("a_kept")
        a_stats = sem("a_stats")
        d_bn = sem("d_bn")
        s_bn = sem("s_bn")
        x_loaded = sem("x_loaded")
        t_done = sem("t_done")
        clip_done = sem("clip_done")
        x1_done = sem("x1_done")
        ph_done = sem("ph_done")
        pl_done = sem("pl_done")
        centre_done = sem("centre_done")
        xc_done = sem("xc_done")
        var_done = sem("var_done")
        sqrt_done = sem("sqrt_done")
        rstd_done = sem("rstd_done")
        u_done = sem("u_done")
        shi_done = sem("shi_done")
        slo_done = sem("slo_done")
        feat_done = sem("feat_done")
        logits_done = sem("logits_done")
        gate_sub = sem("gate_sub")
        gate_exp = sem("gate_exp")
        gate_done = sem("gate_done")
        wb_full = sem("wb_full")
        wb_done = sem("wb_done")
        g_full = sem("g_full")
        g_done = sem("g_done")
        x1g_done = sem("x1g_done")
        d_feat = sem("d_feat")
        d_gate = sem("d_gate")
        z1_full = [sem(f"z1_full{i}") for i in range(2)]
        hhi_done = [sem(f"hhi_done{i}") for i in range(2)]
        hlo_done = [sem(f"hlo_done{i}") for i in range(2)]
        z2_full = [sem(f"z2_full{i}") for i in range(2)]
        v0_done = sem("v0_done")
        relu1_done = sem("relu1_done")
        v1_done = sem("v1_done")
        l3_done = sem("l3_done")
        out_done = sem("out_done")
        stored = [sem(f"stored{i}") for i in range(2)]

        RING2, RINGA, RINGS = 2, GA, 2 * GA

        x_pairs = x.rearrange("b c (k two) w -> b c k two w", two=2)
        N_CW, N_W2, N_FFN = 4, 2 * PAIRS, 21

        def body_of_chunks(eng, chunk):
            with eng.Fori(0, RP // 2 - 1) as j:
                chunk(2 * j, 0, j, False)
                chunk(2 * j + 1, 1, j, False)
            chunk(RP - 2, 0, RP // 2 - 1, False)
            chunk(RP - 1, 1, RP // 2 - 1, True)

        def body_of_images(eng, image):
            with eng.Fori(0, B // XRING - 1) as r:
                for i in range(XRING):
                    image(XRING * r + i, i, r, 0)
            for i in range(XRING):
                image(B - XRING + i, i, B // XRING - 1, XRING - 1 - i)

        with nc.Block() as block:

            @block.sync
            def _(sp):
                for s in stored:
                    sp.sem_inc(s, 16)
                for h in range(2):
                    sp.dma_start(cwt[64 * h:64 * h + 64], cw).then_inc(s_cw, 16)
                    sp.dma_start(gb[64 * h:64 * h + 64, 0:1], gamma.rearrange("(c o) -> c o", o=1)).then_inc(s_cw, 16)

                def load_image(b, slot):
                    xb = x_pairs[b] if isinstance(b, int) else x_pairs[bass.ds(b, 1)].rearrange("o c k t w -> (o c) k t w")
                    sp.dma_start(xa[0:64, slot, 1:SLOTS, :], xb[:, :, 1, :]).then_inc(s_xa[slot], 16)
                    sp.dma_start(xa[64:128, slot, 0:RP, :], xb[:, :, 0, :]).then_inc(s_xa[slot], 16)

                sp.wait_ge(s_zero, 1)
                for b in range(XRING):
                    load_image(b, b)
                with sp.Fori(0, B // XRING - 1) as r:
                    for i in range(XRING):
                        sp.wait_ge(a_split, XRING * r + i + 1)
                        load_image(XRING * r + XRING + i, i)

                def load_chunk(q):
                    xq = x[:, :, bass.ds(2 * q, 2), :] if not isinstance(q, int) else x[:, :, 2 * q:2 * q + 2, :]
                    for h in range(2):
                        sp.dma_start(xin[64 * h:64 * h + 64], xq[:, :, h, :].rearrange("b c w -> c b w")).then_inc(x_loaded, 16)

                sp.wait_ge(s_bn, 1)
                load_chunk(0)
                sp.wait_ge(x1_done, G + RING2)
                load_chunk(1)

                def chunk(k, s, j, last):
                    if not (isinstance(k, int) and k + 2 >= RP):
                        sp.wait_ge(x1_done, G * k + 2 * G + RING2)
                        load_chunk(k + 2)
                    sp.wait_ge(out_done, G * k + G + 1)
                    oq = out[:, :, bass.ds(2 * k, 2), :] if not isinstance(k, int) else out[:, :, 2 * k:2 * k + 2, :]
                    for h in range(2):
                        sp.dma_start(oq[:, :, h, :].rearrange("b c w -> c b w"), o[64 * h:64 * h + 64, s]).then_inc(stored[s], 16)

                body_of_chunks(sp, chunk)
                for s in range(2):
                    sp.wait_ge(stored[s], 32 * (RP // 2) + 16)

            @block.gpsimd
            def _(pool):
                for s, n in ((x1_done, RING2), (u_done, RING2)):
                    pool.sem_inc(s, n)
                nc.gpsimd.memset(ident[:], 0.0).then_inc(s_const, 1)
                nc.gpsimd.memset(halves[:], 0.0).then_inc(s_const, 1)
                nc.gpsimd.memset(ones64[:], 0.0).then_inc(s_const, 1)
                pool.wait_ge(s_const, 3)
                nc.gpsimd.affine_select(out=ident[:], in_=ident[:], compare_op=ALU.not_equal, fill=1.0, base=0,
                                        pattern=[[-1, P]], channel_multiplier=1).then_inc(s_const, 1)
                for n, base in enumerate((0, C, -C)):
                    pool.wait_ge(s_const, 4 + n)
                    nc.gpsimd.affine_select(out=halves[:], in_=halves[:], compare_op=ALU.not_equal, fill=0.5, base=base,
                                            pattern=[[-1, P]], channel_multiplier=1).then_inc(s_const, 1)
                for h in range(2):
                    pool.wait_ge(s_const, 7 + h)
                    nc.gpsimd.memset(ones64[64 * h:64 * h + 64, 64 * h:64 * h + 64], 1.0 / C).then_inc(s_const, 1)

                dma = pool.dma_start
                for i, vec in enumerate((g1, v1, b1, m1, be1, g2, v2)):
                    dma(rows[:, i, :], vec.rearrange("(o e) h -> o (e h)", o=1).broadcast_to([P, E * C])).then_inc(s_ffn, 16)
                for i, vec in enumerate((g2, v2, b2, m2, be2)):
                    dma(cols[:, i, :], vec.rearrange("(q two) h -> (two h) q", two=2), allow_slow_non_contiguous=True).then_inc(s_ffn, 16)
                for h in range(2):
                    dma(wraw[64 * h:64 * h + 64], W1.rearrange("e d h -> d e h")).then_inc(s_ffn, 16)
                dma(wo[:], Wo.rearrange("(q two) h d -> (two h) q d", two=2)).then_inc(s_ffn, 16)
                dma(gb[0:64, 1:2], beta.rearrange("(c o) -> c o", o=1)).then_inc(s_ffn, 16)
                dma(gb[64:128, 1:2], beta.rearrange("(c o) -> c o", o=1)).then_inc(s_ffn, 16)
                for h in range(2):
                    dma(brb[:, h, :], br.rearrange("(o e) -> o e", o=1).broadcast_to([W, E])).then_inc(s_ffn, 16)
                pool.wait_ge(s_zero, 2)
                for h in range(2):
                    dma(wr[64 * h:64 * h + 64, h, :], Wr).then_inc(s_ffn, 16)
                    dma(expert_const[E * h:E * h + E, 64 * h:64 * h + 64], bo).then_inc(s_w2, 16)
                    w2h = W2.rearrange("(q two) h k -> two h q k", two=2)[h]
                    dma(w2raw[64 * h:64 * h + 64, :, 64 * h:64 * h + 64], w2h).then_inc(s_w2, 16)

                def x1(q, s, j, g):
                    if g == 0:
                        pool.wait_ge(x_loaded, 32 * q + 32)
                        pool.wait_ge(stored[s], 32 * j + 16)
                    pool.wait_ge(clip_done, G * q + g + 1)
                    og = o[:, s, BG * g:BG * g + BG, :]
                    nc.gpsimd.tensor_tensor(og, xin[:, BG * g:BG * g + BG, :],
                                            t[:, g % 2].rearrange("p (b w) -> p b w", w=W), ALU.add).then_inc(x1_done, 1)

                def norm(q, g):
                    pool.wait_ge(slo_done, G * q + g + 1)
                    pool.wait_ge(rstd_done, G * q + g + 1)
                    nc.gpsimd.tensor_tensor(u[:, g % 2], xc[:, g % 2], rstd[:, g % 2], ALU.mult).then_inc(u_done, 1)

                def add_const(q, s, g):
                    if g == 0:
                        pool.wait_ge(g_done, q + 2)
                    og = o[:, s, BG * g:BG * g + BG, :]
                    nc.gpsimd.tensor_tensor(og, og, gconst[:, s:s + 1, :].broadcast_to([P, BG, W]), ALU.add).then_inc(x1g_done, 1)

                def prep(q, s, j, n):
                    if n % 2 == 0 and n < 2 * G:
                        x1(q, s, j, n // 2)
                    if n % 2 == 0 and 4 <= n < 4 + 2 * G:
                        norm(q, n // 2 - 2)
                    if n == UNITS - 1:
                        for g in range(G):
                            add_const(q, s, g)

                def chunk(k, s, j, last):
                    for n in range(UNITS):
                        unit = UNITS * k + n
                        if n == 0:
                            pool.wait_ge(wb_done, k + 1)
                        pool.wait_ge(relu1_done, unit + 2)
                        nc.gpsimd.tensor_tensor(v[:, n % 2, 1].rearrange("p (b w) -> p b w", w=W),
                                                v[:, n % 2, 1].rearrange("p (b w) -> p b w", w=W),
                                                wb[:, s, n % PAIRS, 1:2, :].broadcast_to([P, BG, W]),
                                                ALU.mult).then_inc(v1_done, 1)
                        if not last:
                            prep(k + 1, 1 - s, j + s, n)

                for n in range(UNITS):
                    prep(0, 0, 0, n)
                body_of_chunks(pool, chunk)

            @block.tensor
            def _(pe):
                for s, n in ((a_conv, RINGS), (centre_done, RING2), (z2_full[0], RING2), (z2_full[1], RING2), (l3_done, RING2)):
                    pe.sem_inc(s, n)
                mm = nc.tensor.matmul

                pe.wait_ge(s_act, 2)
                for kx in range(3):
                    for n, first in enumerate((1, 0, 3, 2)):
                        at = ps[:, kx // 2, 256 * (kx % 2) + 64 * n:256 * (kx % 2) + 64 * n + 64]
                        last = mm(at, cwsign[:, kx, first:first + 2, :].rearrange("p a c -> p (a c)"), identb[:], start=True, stop=True)
                last.then_inc(s_pe, 1)
                pe.wait_ge(s_dve, 14)
                mm(ps[:, 2], ones64[:], tmp[:], start=True, stop=True).then_inc(s_pe, 1)
                pe.wait_ge(s_dve, 27)
                for q in range(PAIRS):
                    last = mm(ps[0:2 * E, 3, 0:C], c2sel[:, q, :], wo[:, q, :], start=(q == 0), stop=(q == PAIRS - 1))
                last.then_inc(s_pe, 1)
                pe.wait_ge(s_dve, 28)

                def centre_image(b, i):
                    pe.wait_ge(a_split, b + 1)
                    for g in range(GA):
                        lo, hi = slot_group(g)
                        pe.wait_ge(a_signed, GA * b + g + 1)
                        at = ps[:, g, 0:(hi - lo) * W]
                        mm(at, centre[:], xhi[:, i % 2, lo:hi, :], start=True, stop=False)
                        mm(at, centre[:], xlo[:, i % 2, lo:hi, :], start=False, stop=True).then_inc(a_centred, 1)

                def conv_image(b, i):
                    for g in range(GA):
                        pe.wait_ge(a_signed, GA * b + g + 1 + RINGA)
                        pe.wait_ge(a_kept, GA * b + g + 1)
                        at = ps[:, GA + g, 0:KG * W]
                        for kx in range(3):
                            for nxt in range(2):
                                last = mm(at, convw[:, kx, nxt, :], sgn[:, i % 2, KG * g + nxt:KG * g + nxt + KG, kx:kx + W],
                                          start=(kx + nxt == 0), stop=(kx + nxt == 3))
                        last.then_inc(a_conv, 1)

                pe.wait_ge(s_act, 3)
                centre_image(0, 0)

                def image(b, i, r, left):
                    if not isinstance(b, int) or left:
                        centre_image(b + 1, i + 1)
                    conv_image(b, i)

                body_of_images(pe, image)

                for n in range(2):
                    pe.wait_ge(a_stats, B + 1 + 3 * n)
                    mm(ps[:, 0, n:n + 1], halves[:], bn[:, 4 + n:5 + n], start=True, stop=True).then_inc(s_pe, 1)

                def layer1(k, s, n):
                    unit, g, q = UNITS * k + n, n // PAIRS, n % PAIRS
                    if q == 0:
                        pe.wait_ge(slo_done, G * k + g + 1 + RING2)
                    for par in range(2):
                        pe.wait_ge(hlo_done[par], unit + 1)
                        at = ps[:, 2 * (n % 2) + par, 0:NG]
                        mm(at, w1hi[:, P * q:P * q + P], stack[:, s, par, g, :], start=True, stop=False)
                        mm(at, w1lo[:, P * q:P * q + P], stack[:, s, par, g, :], start=False, stop=True).then_inc(z1_full[par], 1)

                def layer2(k, n):
                    unit, q = UNITS * k + n, n % PAIRS
                    for par in range(2):
                        pe.wait_ge(hlo_done[par], unit + 1 + RING2)
                        pe.wait_ge((v0_done, relu1_done)[par], unit + 1)
                        at = ps[:, 4 + par, 0:NG]
                        mm(at, w2hi[:, q, :], hhi[:, n % 2, par, :], start=True, stop=False)
                        mm(at, w2lo[:, q, :], hhi[:, n % 2, par, :], start=False, stop=False)
                        mm(at, w2hi[:, q, :], hlo[:, n % 2, par, :], start=False, stop=True).then_inc(z2_full[par], 1)

                def layer3(k, n):
                    unit, g, q = UNITS * k + n, n // PAIRS, n % PAIRS
                    pe.wait_ge(v0_done, unit + 2)
                    pe.wait_ge(v1_done, unit + 1)
                    if q == 0:
                        pe.wait_ge(out_done, G * k + g + 1)
                    for par in range(2):
                        last = mm(ps[64 * par:64 * par + 64, 6, 0:NG], wo[:, q, :], v[:, n % 2, par, :],
                                  start=(q == 0), stop=(q == PAIRS - 1))
                    last.then_inc(l3_done, 1)

                def prep(q, s, n):
                    g = n // 2 - 1
                    if 2 <= n < 2 + 2 * G and n % 2 == 0:
                        pe.wait_ge(pl_done, G * q + g + 1)
                        pe.wait_ge(sqrt_done, G * q + g + 1)
                        if g == 0:
                            pe.wait_ge(g_done, q + 1)
                        mm(misc[:, 0:NG], centre[:], ph[:, g % 2, :], start=True, stop=False)
                        mm(misc[:, 0:NG], centre[:], pl[:, g % 2, :], start=False, stop=True).then_inc(centre_done, 1)
                    if 2 <= n < 2 + 2 * G and n % 2 == 1:
                        pe.wait_ge(xc_done, G * q + g + 1)
                        mm(misc[:, 0:NG], ones64[:], rstd[:, g % 2, :], start=True, stop=True).then_inc(var_done, 1)
                    if n == 12:
                        pe.wait_ge(feat_done, q + 1)
                        pe.wait_ge(sqrt_done, G * q + G + 1)
                        mm(misc[0:W, 0:2 * E], feat[:], wr[:].rearrange("p a e -> p (a e)"), start=True, stop=True).then_inc(logits_done, 1)
                    if n == 14:
                        pe.wait_ge(gate_done, q + 1)
                        for pair in range(PAIRS):
                            for par in range(2):
                                at = (2 * pair + par) * W
                                for h in range(2):
                                    e = 2 * pair + h
                                    mm(misc[64 * h:64 * h + 64, at:at + W], gate_w[:, par, e:e + 1].broadcast_to([P, C]),
                                       ident[:, 0:W], start=True, stop=True)
                        mm(misc[0:2 * E, NG:NG + W], gate_w[:].rearrange("p a e -> p (a e)"), ident[:, 0:W],
                           start=True, stop=True).then_inc(wb_full, 1)
                    if n == 15:
                        pe.wait_ge(wb_done, q + 1)
                        mm(misc[:, 0:W], expert_const[:], wT[:], start=True, stop=True).then_inc(g_full, 1)

                def chunk(k, s, j, last):
                    for n in range(UNITS):
                        if n + 1 < UNITS:
                            layer1(k, s, n + 1)
                        elif not last:
                            layer1(k + 1, 1 - s, 0)
                        layer2(k, n)
                        if n:
                            layer3(k, n - 1)
                        if not last:
                            prep(k + 1, 1 - s, n)
                    layer3(k, UNITS - 1)

                for n in range(UNITS):
                    prep(0, 0, n)
                layer1(0, 0, 0)
                body_of_chunks(pe, chunk)

            @block.scalar
            def _(act):
                for s, n in ((a_signed, RINGA), (a_kept, RINGA), (relu1_done, 1), (sqrt_done, 1), (g_done, 1)):
                    act.sem_inc(s, n)
                A = nc.scalar.activation
                act.wait_ge(s_dve, 6)
                A(bn[:, 8:9], bn[:, 7:8], ACT.Sqrt, scale=1.0 / (C * TAPS - 1)).then_inc(s_act, 1)
                A(cwsign[:, :, 1:4, :], cwt[0:64].rearrange("p ci ky kx -> p kx ky ci"), ACT.Sign).then_inc(s_act, 1)
                act.wait_ge(s_pe, 1)
                A(convw[:, 0:2].rearrange("p k a m -> p (k a m)"), ps[:, 0, :], ACT.Copy)
                A(convw[:, 2].rearrange("p a m -> p (a m)"), ps[:, 1, 0:256], ACT.Copy).then_inc(s_act, 1)
                act.wait_ge(s_dve, 9)
                A(rows[:, 1, :], rows[:, 1, :], ACT.Sqrt)
                A(rows[:, 6, :], rows[:, 6, :], ACT.Sqrt)
                A(cols[:, 1, :], cols[:, 1, :], ACT.Sqrt).then_inc(s_act, 1)

                def sign_image(b, i):
                    act.wait_ge(a_conv, GA * b + GA)
                    for g in range(GA):
                        lo, hi = slot_group(g)
                        act.wait_ge(a_centred, GA * b + g + 1)
                        A(sgn[:, i % 2, lo:hi, 1:W + 1], ps[:, g, 0:(hi - lo) * W].rearrange("p (k w) -> p k w", w=W),
                          ACT.Sign).then_inc(a_signed, 1)

                def keep_image(b):
                    for g in range(GA):
                        act.wait_ge(a_conv, GA * b + g + 1 + RINGS)
                        yb = y[:, KG * g:KG * g + KG, b, :] if isinstance(b, int) else \
                            y[:, KG * g:KG * g + KG, bass.ds(b, 1), :].rearrange("p k o w -> p (k o) w")
                        A(yb, ps[:, GA + g, 0:KG * W].rearrange("p (k w) -> p k w", w=W), ACT.Copy).then_inc(a_kept, 1)

                act.wait_ge(s_zero, 1)
                sign_image(0, 0)

                def image(b, i, r, left):
                    if not isinstance(b, int) or left:
                        sign_image(b + 1, i + 1)
                    keep_image(b)

                body_of_images(act, image)
                act.wait_ge(a_stats, B + 5)
                A(bn[:, 11:12], bn[:, 10:11], ACT.Sqrt).then_inc(s_act, 1)

                def relu_hi(k, n):
                    unit = UNITS * k + n
                    for par in range(2):
                        act.wait_ge(z1_full[par], unit + 1)
                        act.wait_ge(z2_full[par], unit + 1)
                        A(hhi[:, n % 2, par, :], ps[:, 2 * (n % 2) + par, 0:NG], ACT.Relu).then_inc(hhi_done[par], 1)

                def relu1(k, n):
                    unit = UNITS * k + n
                    act.wait_ge(z2_full[1], unit + 1 + RING2)
                    act.wait_ge(l3_done, unit + 1)
                    A(v[:, n % 2, 1, :], ps[:, 5, 0:NG], ACT.Relu, bias=bias2[:, n % PAIRS:n % PAIRS + 1]).then_inc(relu1_done, 1)

                def prep(q, s, n):
                    if n % 2 == 0 and n < 2 * G:
                        g = n // 2
                        act.wait_ge(x1_done, G * q + g + 1)
                        yq = y[:, q, BG * g:BG * g + BG, :] if isinstance(q, int) else \
                            y[:, bass.ds(q, 1), BG * g:BG * g + BG, :].rearrange("p o b w -> p (o b) w")
                        A(t[:, g % 2].rearrange("p (b w) -> p b w", w=W), yq, ACT.Identity, bias=OFFSET, scale=SCALE).then_inc(t_done, 1)
                    if n % 2 == 1 and n < 2 * G:
                        g = n // 2
                        act.wait_ge(x1_done, G * q + g + 1 + RING2)
                        act.wait_ge(centre_done, G * q + g + 1)
                        A(ph[:, g % 2, :], o[:, s, BG * g:BG * g + BG, :].rearrange("p b w -> p (b w)"), ACT.Copy).then_inc(ph_done, 1)
                    if n % 2 == 0 and 2 <= n < 2 + 2 * G:
                        g = n // 2 - 1
                        act.wait_ge(centre_done, G * q + g + 1 + RING2)
                        act.wait_ge(u_done, G * q + g + 1)
                        A(rstd[:, g % 2, :], misc[:, 0:NG], ACT.Square)
                        A(xc[:, g % 2, :], misc[:, 0:NG], ACT.Copy).then_inc(xc_done, 1)
                    if n % 2 == 1 and 2 <= n < 2 + 2 * G:
                        g = n // 2 - 1
                        act.wait_ge(var_done, G * q + g + 1)
                        A(rstd[:, g % 2, :], misc[:, 0:NG], ACT.Sqrt, bias=LN_EPS).then_inc(sqrt_done, 1)
                    if n % 2 == 1 and 5 <= n < 5 + 2 * G:
                        g = (n - 5) // 2
                        act.wait_ge(u_done, G * q + g + 1 + RING2)
                        for par in range(2):
                            h = slice(64 * par, 64 * par + 64)
                            A(stack[h, s, par, g, :], u[h, g % 2, :], ACT.Copy, bias=SHIFT).then_inc(shi_done, 1)
                    if n == 13:
                        act.wait_ge(gate_sub, q + 1)
                        A(gate_e[:], gate[:], ACT.Exp).then_inc(gate_exp, 1)
                    if n == 14:
                        act.wait_ge(wb_full, q + 1)
                        A(wT[:], misc[0:2 * E, NG:NG + W], ACT.Copy)
                        A(wb[:, s].rearrange("p a b w -> p (a b w)"), misc[:, 0:NG], ACT.Copy).then_inc(wb_done, 1)
                    if n == 15:
                        act.wait_ge(g_full, q + 1)
                        A(gconst[:, s, :], misc[:, 0:W], ACT.Copy).then_inc(g_done, 1)

                def chunk(k, s, j, last):
                    for n in range(UNITS):
                        if n + 1 < UNITS:
                            relu_hi(k, n + 1)
                        elif not last:
                            relu_hi(k + 1, 0)
                        relu1(k, n)
                        if not last:
                            prep(k + 1, 1 - s, n)

                act.wait_ge(s_bn, 1)
                for n in range(UNITS):
                    prep(0, 0, n)
                relu_hi(0, 0)
                body_of_chunks(act, chunk)

            @block.vector
            def _(dve):
                V = nc.vector
                for s, n in ((slo_done, RING2), (hlo_done[0], RING2), (hlo_done[1], RING2), (v0_done, 1), (out_done, 1)):
                    dve.sem_inc(s, n)
                V.memset(xa[:, :, 0:1, :], 0.0)
                V.memset(xa[:, :, RP:SLOTS, :], 0.0)
                V.memset(sgn[:], 0.0).then_inc(s_zero, 1)
                V.memset(w2raw[:], 0.0)
                V.memset(wr[:], 0.0)
                V.memset(expert_const[:], 0.0)
                V.memset(c2sel[:], 0.0)
                V.memset(cwsign[:], 0.0).then_inc(s_zero, 1)

                count = [0]

                def step(ins):
                    count[0] += 1
                    ins.then_inc(s_dve, 1)
                    dve.wait_ge(s_dve, count[0])

                dve.wait_ge(s_cw, 16 * N_CW)
                dve.wait_ge(s_zero, 2)
                cflat = cwt[:].rearrange("p a b c -> p (a b c)")
                step(V.tensor_reduce(bn[:, 3:4], cflat, AX.X, ALU.add))
                step(V.tensor_scalar(bn[:, 3:4], bn[:, 3:4], 1.0 / (C * TAPS), None, ALU.mult))
                step(V.tensor_scalar(cflat, cflat, bn[:, 3:4], None, ALU.subtract))
                step(V.tensor_tensor(cwa[:], cflat, cflat, ALU.mult))
                step(V.tensor_reduce(bn[:, 7:8], cwa[:], AX.X, ALU.add))
                dve.wait_ge(s_const, 9)
                step(V.tensor_copy(identb[:], ident[0:64, 0:64]))
                step(V.scalar_tensor_tensor(out=cwa[:], in0=cflat, scalar=-1.0, in1=cflat, op0=ALU.mult, op1=ALU.max))
                step(V.tensor_reduce(bn[:, 9:10], cwa[:], AX.X, ALU.add))

                dve.wait_ge(s_ffn, 16 * N_FFN)
                V.tensor_scalar(rows[:, 1, :], rows[:, 1, :], BNF_EPS, None, ALU.add)
                V.tensor_scalar(rows[:, 6, :], rows[:, 6, :], BNF_EPS, None, ALU.add)
                step(V.tensor_scalar(cols[:, 1, :], cols[:, 1, :], BNF_EPS, None, ALU.add))
                V.tensor_tensor(rows[:, 2, :], rows[:, 2, :], rows[:, 3, :], ALU.subtract)
                V.tensor_tensor(cols[:, 2, :], cols[:, 2, :], cols[:, 3, :], ALU.subtract)
                V.tensor_tensor(centre[:], ident[:], ones64[:], ALU.subtract)

                dve.wait_ge(s_act, 1)
                step(V.reciprocal(SW, bn[:, 8:9]))
                step(V.tensor_scalar(bn[:, 9:10], bn[:, 9:10], SW, SQRT2 / (C * TAPS), ALU.mult, ALU.mult))
                step(V.tensor_scalar(SW.bitcast(I32), bn[:, 9:10].bitcast(I32), EXP_MASK, None, ALU.bitwise_and))

                dve.wait_ge(s_act, 4)
                V.reciprocal(rows[:, 6, :], rows[:, 6, :])
                V.reciprocal(cols[:, 1, :], cols[:, 1, :])
                step(V.reciprocal(rows[:, 1, :], rows[:, 1, :]))
                r1 = lambda i: rows[:, i, :]
                V.tensor_tensor(r1(6), r1(6), r1(5), ALU.mult)
                V.tensor_tensor(cols[:, 1, :], cols[:, 1, :], cols[:, 0, :], ALU.mult)
                V.tensor_tensor(r1(1), r1(1), r1(0), ALU.mult)
                V.memset(cols[:, 5, :], 0.0)
                dve.drain()
                step(V.tensor_tensor(tmp[:], wraw[:].rearrange("p e h -> p (e h)"), r1(1), ALU.mult))
                step(V.tensor_tensor(r1(2), r1(2), r1(1), ALU.mult))
                step(V.tensor_tensor(r1(2), r1(2), r1(4), ALU.add))
                dve.wait_ge(s_pe, 2)
                step(V.scalar_tensor_tensor(out=r1(2), in0=r1(2), scalar=1.0 / (C * SHIFT), in1=ps[:, 2], op0=ALU.mult, op1=ALU.subtract))
                step(V.tensor_tensor(tmp[:], tmp[:], r1(2), ALU.add))
                step(V.tensor_copy(w1hi[:], tmp[:]))
                step(V.tensor_tensor(w1lo[:], tmp[:], w1hi[:].bitcast(F32), ALU.subtract))
                dve.wait_ge(s_w2, 16 * 4)
                w2f = w2raw[:].rearrange("p q m -> p (q m)")
                step(V.tensor_tensor(w2f, w2f, r1(6), ALU.mult))
                step(V.tensor_copy(w2hi[:].rearrange("p q m -> p (q m)"), w2f))
                step(V.tensor_tensor(w2lo[:].rearrange("p q m -> p (q m)"), w2f, w2hi[:].rearrange("p q m -> p (q m)").bitcast(F32), ALU.subtract))
                step(V.tensor_tensor(cols[:, 2, :], cols[:, 2, :], cols[:, 1, :], ALU.mult))
                step(V.tensor_tensor(bias2[:], cols[:, 2, :], cols[:, 4, :], ALU.add))
                V.tensor_scalar(wr[:], wr[:], 1.0 / B, None, ALU.mult)
                step(V.tensor_scalar(negb2[:], bias2[:], -1.0, None, ALU.mult))
                for q in range(PAIRS):
                    V.tensor_copy(c2sel[0:64, q, 2 * q:2 * q + 1], bias2[0:64, q:q + 1])
                    last = V.tensor_copy(c2sel[64:128, q, 2 * q + 1:2 * q + 2], bias2[64:128, q:q + 1])
                step(last)
                dve.wait_ge(s_pe, 3)
                step(V.tensor_tensor(expert_const[:, 0:C], expert_const[:, 0:C], ps[0:2 * E, 3, 0:C], ALU.add))

                def split(b, i, r):
                    s4 = i % XRING
                    dve.wait_ge(s_xa[s4], 32 * (r + i // XRING) + 32)
                    if not (isinstance(b, int) and b < 2):
                        dve.wait_ge(a_centred, GA * b - GA)
                    V.tensor_copy(xhi[:, i % 2], xa[:, s4]).then_inc(a_hi, 1)
                    dve.wait_ge(a_hi, b + 1)
                    V.tensor_tensor(xlo[:, i % 2], xa[:, s4], xhi[:, i % 2].bitcast(F32), ALU.subtract).then_inc(a_split, 1)

                def image_stats(b):
                    for g in range(GA):
                        dve.wait_ge(a_kept, GA * b + g + 1 + RINGA)
                        k = slice(KG * g, KG * g + KG)
                        if isinstance(b, int):
                            yb, sb_ = y[:, k, b, :], stats[:, b, g, :]
                        else:
                            yb = y[:, k, bass.ds(b, 1), :].rearrange("p k o w -> p (k o) w")
                            sb_ = stats[:, bass.ds(b, 1), g, :].rearrange("p o s -> p (o s)")
                        last = V.bn_stats(sb_, yb)
                    last.then_inc(a_stats, 1)

                split(0, 0, 0)
                split(1, 1, 0)

                def image(b, i, r, left):
                    if not isinstance(b, int) or left >= 2:
                        split(b + 2, i + 2, r)
                    image_stats(b)

                body_of_images(dve, image)

                mean, var = bn[:, 12:13], bn[:, 13:14]
                dve.wait_ge(a_stats, B)
                V.bn_aggr(bn[:, 4:6], stats[:].rearrange("p b g s -> p (b g s)")).then_inc(a_stats, 1)
                dve.wait_ge(s_pe, 4)
                V.tensor_copy(mean, ps[:, 0, 0:1]).then_inc(a_stats, 1)
                dve.wait_ge(a_stats, B + 2)
                V.tensor_tensor(bn[:, 14:15], bn[:, 4:5], mean, ALU.subtract).then_inc(a_stats, 1)
                dve.wait_ge(a_stats, B + 3)
                V.scalar_tensor_tensor(out=bn[:, 5:6], in0=bn[:, 14:15], scalar=bn[:, 14:15], in1=bn[:, 5:6],
                                       op0=ALU.mult, op1=ALU.add).then_inc(a_stats, 1)
                dve.wait_ge(s_pe, 5)
                V.tensor_scalar(bn[:, 13:14], ps[:, 0, 1:2], SW, None, ALU.mult).then_inc(d_bn, 1)
                dve.wait_ge(d_bn, 1)
                V.tensor_scalar(bn[:, 10:11], var, SW, BN1_EPS, ALU.mult, ALU.add).then_inc(a_stats, 1)
                dve.wait_ge(s_act, 5)
                V.reciprocal(bn[:, 15:16], bn[:, 11:12]).then_inc(d_bn, 1)
                dve.wait_ge(d_bn, 2)
                V.tensor_scalar(bn[:, 14:15], bn[:, 15:16], SW, None, ALU.mult).then_inc(d_bn, 1)
                dve.wait_ge(d_bn, 3)
                V.tensor_scalar(SCALE, bn[:, 14:15], gb[:, 0:1], None, ALU.mult).then_inc(d_bn, 1)
                dve.wait_ge(d_bn, 4)
                V.tensor_scalar(bn[:, 14:15], mean, SCALE, None, ALU.mult).then_inc(d_bn, 1)
                dve.wait_ge(d_bn, 5)
                V.tensor_tensor(OFFSET, gb[:, 1:2], bn[:, 14:15], ALU.subtract).then_inc(s_bn, 1)

                def relu_lo(k, n):
                    unit = UNITS * k + n
                    for par in range(2):
                        dve.wait_ge(hhi_done[par], unit + 1)
                        V.scalar_tensor_tensor(out=hlo[:, n % 2, par, :], in0=ps[:, 2 * (n % 2) + par, 0:NG], scalar=0.0,
                                               in1=hhi[:, n % 2, par, :].bitcast(F32), op0=ALU.max, op1=ALU.subtract).then_inc(hlo_done[par], 1)

                def v0(k, s, n):
                    unit, q = UNITS * k + n, n % PAIRS
                    if n == 0:
                        dve.wait_ge(wb_done, k + 1)
                    dve.wait_ge(z2_full[0], unit + 1 + RING2)
                    dve.wait_ge(l3_done, unit + 1)
                    V.scalar_tensor_tensor(out=v[:, n % 2, 0, :].rearrange("p (b w) -> p b w", w=W),
                                           in0=ps[:, 4, 0:NG].rearrange("p (b w) -> p b w", w=W), scalar=negb2[:, q:q + 1],
                                           in1=wb[:, s, q, 0:1, :].broadcast_to([P, BG, W]),
                                           op0=ALU.max, op1=ALU.mult).then_inc(v0_done, 1)

                def add_out(k, s, g):
                    dve.wait_ge(l3_done, UNITS * k + PAIRS * g + PAIRS + RING2)
                    dve.wait_ge(x1g_done, G * k + g + 1)
                    og = o[:, s, BG * g:BG * g + BG, :].rearrange("p b w -> p (b w)")
                    V.tensor_tensor(og, ps[:, 6, 0:NG], og, ALU.add).then_inc(out_done, 1)

                GATE_STEPS = 4

                def prep(q, s, n):
                    if n % 2 == 0 and n < 2 * G:
                        g = n // 2
                        dve.wait_ge(t_done, G * q + g + 1)
                        V.tensor_scalar(t[:, g % 2, :], t[:, g % 2, :], 1.0, -1.0, ALU.min, ALU.max).then_inc(clip_done, 1)
                    if n % 2 == 1 and n < 2 * G:
                        g = n // 2
                        dve.wait_ge(ph_done, G * q + g + 1)
                        V.tensor_tensor(pl[:, g % 2, :], o[:, s, BG * g:BG * g + BG, :].rearrange("p b w -> p (b w)"),
                                        ph[:, g % 2, :].bitcast(F32), ALU.subtract).then_inc(pl_done, 1)
                    if n % 2 == 1 and 2 <= n < 2 + 2 * G:
                        g = n // 2 - 1
                        dve.wait_ge(sqrt_done, G * q + g + 2)
                        V.reciprocal(rstd[:, g % 2, :], rstd[:, g % 2, :]).then_inc(rstd_done, 1)
                    if n % 2 == 1 and 5 <= n < 5 + 2 * G:
                        g = (n - 5) // 2
                        dve.wait_ge(u_done, G * q + g + 1 + RING2)
                        V.tensor_reduce(feat4[:, g, :], u[:, g % 2, :].rearrange("p (b w) -> p w b", w=W), AX.X, ALU.add).then_inc(d_feat, 1)
                        for par in range(2):
                            h = slice(64 * par, 64 * par + 64)
                            other = slice(64 - 64 * par, 128 - 64 * par)
                            dve.wait_ge(shi_done, 2 * (G * q + g) + par + 1)
                            last = V.scalar_tensor_tensor(out=stack[other, s, par, g, :], in0=u[h, g % 2, :], scalar=SHIFT,
                                                          in1=stack[h, s, par, g, :].bitcast(F32), op0=ALU.add, op1=ALU.subtract)
                        last.then_inc(slo_done, 1)
                    if n == 11:
                        dve.wait_ge(d_feat, G * q + G)
                        V.tensor_reduce(feat[:], feat4[:].rearrange("p g w -> p w g"), AX.X, ALU.add).then_inc(feat_done, 1)
                    if n == 12:
                        dve.wait_ge(logits_done, q + 1)
                        V.tensor_tensor(gate[:].rearrange("p a e -> p (a e)"), misc[0:W, 0:2 * E], brb[:].rearrange("p a e -> p (a e)"), ALU.add).then_inc(d_gate, 1)
                        dve.wait_ge(d_gate, GATE_STEPS * q + 1)
                        V.tensor_reduce(gate_s[:, :, 0:1], gate[:], AX.X, ALU.max).then_inc(d_gate, 1)
                        dve.wait_ge(d_gate, GATE_STEPS * q + 2)
                        V.tensor_tensor(gate[:], gate[:], gate_s[:, :, 0:1].broadcast_to([W, 2, E]), ALU.subtract).then_inc(gate_sub, 1)
                    if n == 13:
                        dve.wait_ge(gate_exp, q + 1)
                        V.tensor_reduce(gate_s[:, :, 0:1], gate_e[:], AX.X, ALU.add).then_inc(d_gate, 1)
                        dve.wait_ge(d_gate, GATE_STEPS * q + 3)
                        V.reciprocal(gate_s[:, :, 1:2], gate_s[:, :, 0:1]).then_inc(d_gate, 1)
                        dve.wait_ge(d_gate, GATE_STEPS * q + 4)
                        V.tensor_tensor(gate_w[0:W], gate_e[:], gate_s[:, :, 1:2].broadcast_to([W, 2, E]), ALU.mult).then_inc(gate_done, 1)

                def chunk(k, s, j, last):
                    for n in range(UNITS):
                        if n + 1 < UNITS:
                            relu_lo(k, n + 1)
                        elif not last:
                            relu_lo(k + 1, 0)
                        if n % PAIRS == 0 and n:
                            add_out(k, s, n // PAIRS - 1)
                        v0(k, s, n)
                        if not last:
                            prep(k + 1, 1 - s, n)
                    add_out(k, s, G - 1)

                V.memset(gate_w[:], 0.0).then_inc(d_bn, 1)
                dve.wait_ge(d_bn, 6)
                for n in range(UNITS):
                    prep(0, 0, n)
                relu_lo(0, 0)
                body_of_chunks(dve, chunk)
        late.close()


_INS = ["x", "L0_conv_weight", "L0_conv_gamma", "L0_conv_beta", "L0_ffn_Wr", "L0_ffn_br", "L0_ffn_W1", "L0_ffn_b1",
        "L0_ffn_g1", "L0_ffn_be1", "L0_ffn_m1", "L0_ffn_v1", "L0_ffn_W2", "L0_ffn_b2", "L0_ffn_g2", "L0_ffn_be2",
        "L0_ffn_m2", "L0_ffn_v2", "L0_ffn_Wo", "L0_ffn_bo"]


def kernel(**inputs):
    import numpy as _np
    import concourse.bacc as _bacc
    from concourse.bass_utils import run_bass_kernel_spmd as _run

    nc = _bacc.Bacc("TRN2", target_bir_lowering=False, num_devices=1)
    arrays, args = {}, []
    for name in _INS:
        a = _np.ascontiguousarray(inputs[name])
        arrays[f"in_{name}"] = a
        args.append(nc.dram_tensor(f"in_{name}", a.shape, mybir.dt.from_np(a.dtype), kind="ExternalInput").ap())
    args.append(nc.dram_tensor("out", (B, C, H, W), F32, kind="ExternalOutput").ap())
    metaformer_kernel(nc, *args)
    r = _run(nc, [arrays], core_ids=[0])
    return r.results[0]["out"]
```

```python
from contextlib import ExitStack

import concourse.bass as bass
from concourse import mybir

F32 = mybir.dt.float32
F32R = mybir.dt.float32r
F16 = mybir.dt.float16
BF16 = mybir.dt.bfloat16
I32 = mybir.dt.int32
ALU = mybir.AluOpType
ACT = mybir.ActivationFunctionType
AX = mybir.AxisListType

P = 128
B, C, H, W = 32, 64, 56, 56
E = 8
PAIRS = E // 2
RP = H // 2
SLOTS = RP + 1
TAPS = 9
GA = 4
KG = RP // GA
XRING = 4
G = 4
BG = B // G
NG = BG * W
UNITS = G * PAIRS
LN_EPS, BN1_EPS, BNF_EPS = 1e-5, 1e-5, 1e-3
SHIFT = 0.125
EXP_MASK = 0x7F800000
SQRT2 = 2.0 ** 0.5


def slot_group(i):
    return (0 if i == 0 else KG * i + 1), KG * (i + 1) + 1


def metaformer_kernel(nc, x, cw, gamma, beta, Wr, br, W1, b1, g1, be1, m1, v1, W2, b2, g2, be2, m2, v2, Wo, bo, out):
    with ExitStack() as ctx:
        def sb(name, shape, dt, to=ctx):
            return to.enter_context(nc.sbuf_tensor(name, shape, dt))

        def sem(name):
            return ctx.enter_context(nc.semaphore(name))

        y = sb("y", [P, RP, B, W], F16)
        ident = sb("ident", [P, P], F32)
        ones64 = sb("ones64", [P, P], F32)
        centre = sb("centre", [P, P], F32R)
        var_ones = sb("var_ones", [P, 32], F32)
        spread = sb("spread", [P, P], F32R)
        halves = sb("halves", [P, P], F32)
        convw = sb("convw", [P, 3, 2, P], BF16)
        w1hi = sb("w1hi", [P, E * C], F32R)
        w1lo = sb("w1lo", [P, E * C], F32R)
        w2hi = sb("w2hi", [P, PAIRS, P], F32R)
        w2lo = sb("w2lo", [P, PAIRS, P], F32R)
        wo = sb("wo", [P, PAIRS, C], F32)
        wr = sb("wr", [P, 2, E], F32)
        brb = sb("brb", [W, 2, E], F32)
        bias2 = sb("bias2", [P, PAIRS], F32)
        negb2 = sb("negb2", [P, PAIRS], F32)
        expert_const = sb("expert_const", [2 * E, P], F32)
        bn = sb("bn", [P, 16], F32)
        SCALE, OFFSET, SW = bn[:, 0:1], bn[:, 1:2], bn[:, 2:3]
        gb = sb("gb", [P, 2], F32)

        fold = ExitStack()
        rows = sb("rows", [P, 7, E * C], F32, fold)
        cols = sb("cols", [P, 6, PAIRS], F32, fold)
        wraw = sb("wraw", [P, E, C], F32, fold)
        w2raw = sb("w2raw", [P, PAIRS, P], F32, fold)
        c2sel = sb("c2sel", [P, PAIRS, 2 * E], F32, fold)
        tmp = sb("tmp", [P, E * C], F32, fold)
        fold.close()
        hhi = sb("hhi", [P, 2, 2, NG], F32R)
        hlo = sb("hlo", [P, 2, 2, NG], F32R)
        v = sb("v", [P, 2, 2, NG], F32)

        early = ExitStack()
        xa = sb("xa", [P, XRING, SLOTS, W], F32, early)
        xhi = sb("xhi", [P, 2, SLOTS, W], F32R, early)
        xlo = sb("xlo", [P, 2, SLOTS, W], F32R, early)
        sgn = sb("sgn", [P, 2, SLOTS, W + 2], BF16, early)
        stats = sb("stats", [P, B, GA, 6], F32, early)
        cwt = sb("cwt", [P, C, 3, 3], F32, early)
        cwa = sb("cwa", [P, C * TAPS], F32, early)
        cwsign = sb("cwsign", [C, 3, 5, C], BF16, early)
        identb = sb("identb", [C, C], BF16, early)
        early.close()

        xin = sb("xin", [P, B, W], F32)
        o = sb("o", [P, 2, B, W], F32)
        t = sb("t", [P, G, NG], F32)
        ph = sb("ph", [P, 2, NG], F32R)
        pl = sb("pl", [P, 2, NG], F32R)
        xc = sb("xc", [P, G, NG], F32)
        rs = sb("rs", [P, NG], F32)
        rhi = sb("rhi", [P, NG], F32R)
        rlo = sb("rlo", [P, NG], F32R)
        feat4 = sb("feat4", [P, G, W], F32)
        feat = sb("feat", [P, W], F32)
        stack = sb("stack", [P, 2, G, NG], F32R)
        gate = sb("gate", [W, 2, E], F32)
        gate_e = sb("gate_e", [W, 2, E], F32)
        gate_w = sb("gate_w", [P, 2, E], F32)
        gate_s = sb("gate_s", [W, 2, 2], F32)
        wT = sb("wT", [2 * E, W], F32)
        wb = sb("wb", [P, 2, PAIRS, 2, W], F32)
        gconst = sb("gconst", [P, 2, W], F32)

        ps = ctx.enter_context(nc.psum_tensor("ps", [P, 8, 512], F32))
        misc = ps[:, 7]

        s_cw = sem("s_cw")
        s_ffn = sem("s_ffn")
        s_w2 = sem("s_w2")
        s_const = sem("s_const")
        s_zero = sem("s_zero")
        s_dve = sem("s_dve")
        s_act = sem("s_act")
        s_pe = sem("s_pe")
        s_xa = [sem(f"s_xa{i}") for i in range(XRING)]
        a_hi = sem("a_hi")
        a_split = sem("a_split")
        a_centred = sem("a_centred")
        a_signed = sem("a_signed")
        a_conv = sem("a_conv")
        a_kept = sem("a_kept")
        a_stats = sem("a_stats")
        d_bn = sem("d_bn")
        s_bn = sem("s_bn")
        x_loaded = sem("x_loaded")
        t_done = sem("t_done")
        clip_done = sem("clip_done")
        x1_done = sem("x1_done")
        ph_done = sem("ph_done")
        pl_done = sem("pl_done")
        centre_done = sem("centre_done")
        xc_done = sem("xc_done")
        var_done = sem("var_done")
        sqrt_done = sem("sqrt_done")
        rs_done = sem("rs_done")
        d_rs = sem("d_rs")
        rb_full = sem("rb_full")
        rb_done = sem("rb_done")
        u_done = sem("u_done")
        shi_done = sem("shi_done")
        slo_done = sem("slo_done")
        feat_done = sem("feat_done")
        logits_done = sem("logits_done")
        gate_sub = sem("gate_sub")
        gate_exp = sem("gate_exp")
        gate_done = sem("gate_done")
        wb_full = sem("wb_full")
        wb_done = sem("wb_done")
        g_full = sem("g_full")
        g_done = sem("g_done")
        x1g_done = sem("x1g_done")
        d_feat = sem("d_feat")
        d_gate = sem("d_gate")
        z1_full = [sem(f"z1_full{i}") for i in range(2)]
        hhi_done = [sem(f"hhi_done{i}") for i in range(2)]
        hlo_done = [sem(f"hlo_done{i}") for i in range(2)]
        z2_full = [sem(f"z2_full{i}") for i in range(2)]
        v0_done = sem("v0_done")
        relu1_done = sem("relu1_done")
        v1_done = sem("v1_done")
        l3_done = sem("l3_done")
        out_done = sem("out_done")
        stored = [[sem(f"stored{i}_{g}") for g in range(G)] for i in range(2)]

        RING2, RINGA, RINGS = 2, GA, 2 * GA

        x_pairs = x.rearrange("b c (k two) w -> b c k two w", two=2)
        N_CW, N_W2, N_FFN = 4, 4, 21
        DVE_VAR = 13
        DVE_TMP = 16
        DVE_C2SEL = 29
        DVE_ALL = 30

        AT_T = (0, 1, 3, 5)
        AT_SPLIT = (2, 4, 6, 8)
        AT_CENTRE = (4, 6, 8, 10)
        AT_VAR = 12
        AT_INV = (14, 15, 16, 17)
        AT_SPREAD = (18, 19, 20, 21)
        AT_FEAT = (20, 21, 22, 23)
        AT_STACK = (20, 22, 24, 28)
        AT_LOGITS, AT_EXP, AT_GATE, AT_WB, AT_WBC, AT_G, AT_GC = 24, 25, 26, 27, 28, 29, 30

        def body_of_chunks(eng, chunk):
            with eng.Fori(0, RP // 2 - 1) as j:
                chunk(2 * j, 0, j, False)
                chunk(2 * j + 1, 1, j, False)
            chunk(RP - 2, 0, RP // 2 - 1, False)
            chunk(RP - 1, 1, RP // 2 - 1, True)

        def body_of_images(eng, image, between=lambda: None):
            with eng.Fori(0, B // XRING - 1) as r:
                for i in range(XRING):
                    image(XRING * r + i, i, r, 0)
            between()
            for i in range(XRING):
                image(B - XRING + i, i, B // XRING - 1, XRING - 1 - i)

        with nc.Block() as block:

            @block.sync
            def _(sp):
                for s in stored[0] + stored[1]:
                    sp.sem_inc(s, 16)
                for h in range(2):
                    sp.dma_start(cwt[64 * h:64 * h + 64], cw).then_inc(s_cw, 16)
                    sp.dma_start(gb[64 * h:64 * h + 64, 0:1], gamma.rearrange("(c o) -> c o", o=1)).then_inc(s_cw, 16)

                def load_image(b, slot):
                    xb = x_pairs[b] if isinstance(b, int) else x_pairs[bass.ds(b, 1)].rearrange("o c k t w -> (o c) k t w")
                    sp.dma_start(xa[0:64, slot, 1:SLOTS, :], xb[:, :, 1, :]).then_inc(s_xa[slot], 16)
                    sp.dma_start(xa[64:128, slot, 0:RP, :], xb[:, :, 0, :]).then_inc(s_xa[slot], 16)

                sp.wait_ge(s_zero, 1)
                for b in range(XRING):
                    load_image(b, b)
                with sp.Fori(0, B // XRING - 1) as r:
                    for i in range(XRING):
                        sp.wait_ge(a_split, XRING * r + i + 1)
                        load_image(XRING * r + XRING + i, i)

                def load_chunk(q):
                    xq = x[:, :, bass.ds(2 * q, 2), :] if not isinstance(q, int) else x[:, :, 2 * q:2 * q + 2, :]
                    for h in range(2):
                        sp.dma_start(xin[64 * h:64 * h + 64], xq[:, :, h, :].rearrange("b c w -> c b w")).then_inc(x_loaded, 16)

                sp.wait_ge(s_bn, 1)
                load_chunk(0)
                sp.wait_ge(x1_done, G + RING2)
                load_chunk(1)

                def chunk(k, s, j, last):
                    if not (isinstance(k, int) and k + 2 >= RP):
                        sp.wait_ge(x1_done, G * k + 2 * G + RING2)
                        load_chunk(k + 2)
                    oq = out[:, :, bass.ds(2 * k, 2), :] if not isinstance(k, int) else out[:, :, 2 * k:2 * k + 2, :]
                    for g in range(G):
                        images = slice(BG * g, BG * g + BG)
                        sp.wait_ge(out_done, G * k + g + 2)
                        for h in range(2):
                            sp.dma_start(oq[images, :, h, :].rearrange("b c w -> c b w"),
                                         o[64 * h:64 * h + 64, s, images]).then_inc(stored[s][g], 16)

                body_of_chunks(sp, chunk)
                for s in stored[0] + stored[1]:
                    sp.wait_ge(s, 32 * (RP // 2) + 16)

            @block.gpsimd
            def _(pool):
                for s, n in ((x1_done, RING2), (u_done, G)):
                    pool.sem_inc(s, n)
                nc.gpsimd.memset(ident[:], 0.0).then_inc(s_const, 1)
                nc.gpsimd.memset(halves[:], 0.0).then_inc(s_const, 1)
                nc.gpsimd.memset(ones64[:], 0.0)
                nc.gpsimd.memset(var_ones[:], 0.0)
                nc.gpsimd.memset(tmp[:, 0:P], 0.0).then_inc(s_const, 1)
                pool.wait_ge(s_const, 3)
                nc.gpsimd.affine_select(out=ident[:], in_=ident[:], compare_op=ALU.not_equal, fill=1.0, base=0,
                                        pattern=[[-1, P]], channel_multiplier=1).then_inc(s_const, 1)
                for n, base in enumerate((0, C, -C)):
                    pool.wait_ge(s_const, 4 + n)
                    nc.gpsimd.affine_select(out=halves[:], in_=halves[:], compare_op=ALU.not_equal, fill=0.5, base=base,
                                            pattern=[[-1, P]], channel_multiplier=1).then_inc(s_const, 1)
                for h in range(2):
                    pool.wait_ge(s_const, 7 + h)
                    nc.gpsimd.memset(ones64[64 * h:64 * h + 64, 64 * h:64 * h + 64], 1.0 / C).then_inc(s_const, 1)
                for h in range(2):
                    pool.wait_ge(s_const, 9 + h)
                    nc.gpsimd.memset(var_ones[64 * h:64 * h + 64, h:h + 1], 1.0 / C).then_inc(s_const, 1)
                for g in range(G):
                    pool.wait_ge(s_const, 11 + g)
                    nc.gpsimd.affine_select(out=tmp[:, 0:P].rearrange("p (h m) -> p h m", h=2), in_=tmp[:, 0:P].rearrange("p (h m) -> p h m", h=2),
                                            compare_op=ALU.not_equal, fill=1.0, base=-32 * g,
                                            pattern=[[-1, 2], [0, C]], channel_multiplier=1).then_inc(s_const, 1)

                dma = pool.dma_start
                for i, vec in enumerate((g1, v1, b1, m1, be1, g2, v2)):
                    dma(rows[:, i, :], vec.rearrange("(o e) h -> o (e h)", o=1).broadcast_to([P, E * C])).then_inc(s_ffn, 16)
                for i, vec in enumerate((g2, v2, b2, m2, be2)):
                    dma(cols[:, i, :], vec.rearrange("(q two) h -> (two h) q", two=2), allow_slow_non_contiguous=True).then_inc(s_ffn, 16)
                for h in range(2):
                    dma(wraw[64 * h:64 * h + 64], W1.rearrange("e d h -> d e h")).then_inc(s_ffn, 16)
                dma(wo[:], Wo.rearrange("(q two) h d -> (two h) q d", two=2)).then_inc(s_ffn, 16)
                dma(gb[0:64, 1:2], beta.rearrange("(c o) -> c o", o=1)).then_inc(s_ffn, 16)
                dma(gb[64:128, 1:2], beta.rearrange("(c o) -> c o", o=1)).then_inc(s_ffn, 16)
                for h in range(2):
                    dma(brb[:, h, :], br.rearrange("(o e) -> o e", o=1).broadcast_to([W, E])).then_inc(s_ffn, 16)
                pool.wait_ge(s_zero, 2)
                for h in range(2):
                    dma(wr[64 * h:64 * h + 64, h, :], Wr).then_inc(s_ffn, 16)
                    dma(expert_const[E * h:E * h + E, 64 * h:64 * h + 64], bo).then_inc(s_w2, 16)
                    w2h = W2.rearrange("(q two) h k -> two h q k", two=2)[h]
                    dma(w2raw[64 * h:64 * h + 64, :, 64 * h:64 * h + 64], w2h).then_inc(s_w2, 16)

                def x1(q, s, j, g):
                    if g == 0:
                        pool.wait_ge(x_loaded, 32 * q + 32)
                    pool.wait_ge(stored[s][g], 32 * j + 16)
                    pool.wait_ge(clip_done, G * q + g + 1)
                    og = o[:, s, BG * g:BG * g + BG, :]
                    nc.gpsimd.tensor_tensor(og, xin[:, BG * g:BG * g + BG, :],
                                            t[:, g].rearrange("p (b w) -> p b w", w=W), ALU.add).then_inc(x1_done, 1)

                def norm(q, g):
                    pool.wait_ge(rb_done, G * q + g + 1)
                    nc.gpsimd.tensor_tensor(xc[:, g], xc[:, g], t[:, g], ALU.mult).then_inc(u_done, 1)

                def add_const(k, s, g):
                    if g == 0:
                        pool.wait_ge(g_done, k + 2)
                    og = o[:, s, BG * g:BG * g + BG, :]
                    nc.gpsimd.tensor_tensor(og, og, gconst[:, s:s + 1, :].broadcast_to([P, BG, W]), ALU.add).then_inc(x1g_done, 1)

                def prep(q, s, j, h):
                    if h in AT_T:
                        x1(q, s, j, AT_T.index(h))
                    if h - 1 in AT_SPREAD:
                        norm(q, AT_SPREAD.index(h - 1))

                def chunk(k, s, j, last):
                    for n in range(UNITS):
                        unit = UNITS * k + n
                        if not last:
                            prep(k + 1, 1 - s, j + s, 2 * n)
                        if n == 0:
                            pool.wait_ge(wb_done, k + 1)
                        pool.wait_ge(relu1_done, unit + 2)
                        nc.gpsimd.tensor_tensor(v[:, n % 2, 1].rearrange("p (b w) -> p b w", w=W),
                                                v[:, n % 2, 1].rearrange("p (b w) -> p b w", w=W),
                                                wb[:, s, n % PAIRS, 1:2, :].broadcast_to([P, BG, W]),
                                                ALU.mult).then_inc(v1_done, 1)
                        if n % PAIRS == 1:
                            add_const(k, s, n // PAIRS)
                        if not last:
                            prep(k + 1, 1 - s, j + s, 2 * n + 1)

                for h in range(2 * UNITS):
                    prep(0, 0, 0, h)
                body_of_chunks(pool, chunk)

            @block.tensor
            def _(pe):
                for s, n in ((a_conv, RINGS), (centre_done, RING2), (z2_full[0], RING2), (z2_full[1], RING2), (l3_done, RING2)):
                    pe.sem_inc(s, n)
                mm = nc.tensor.matmul

                pe.wait_ge(s_act, 2)
                for kx in range(3):
                    for n, first in enumerate((1, 0, 3, 2)):
                        at = ps[:, kx // 2, 256 * (kx % 2) + 64 * n:256 * (kx % 2) + 64 * n + 64]
                        last = mm(at, cwsign[:, kx, first:first + 2, :].rearrange("p a c -> p (a c)"), identb[:], start=True, stop=True)
                last.then_inc(s_pe, 1)
                def centre_image(b, i):
                    pe.wait_ge(a_split, b + 1)
                    for g in range(GA):
                        lo, hi = slot_group(g)
                        pe.wait_ge(a_signed, GA * b + g + 1)
                        at = ps[:, g, 0:(hi - lo) * W]
                        mm(at, centre[:], xhi[:, i % 2, lo:hi, :], start=True, stop=False)
                        mm(at, centre[:], xlo[:, i % 2, lo:hi, :], start=False, stop=True).then_inc(a_centred, 1)

                def conv_image(b, i):
                    for g in range(GA):
                        pe.wait_ge(a_signed, GA * b + g + 1 + RINGA)
                        pe.wait_ge(a_kept, GA * b + g + 1)
                        at = ps[:, GA + g, 0:KG * W]
                        for kx in range(3):
                            for nxt in range(2):
                                last = mm(at, convw[:, kx, nxt, :], sgn[:, i % 2, KG * g + nxt:KG * g + nxt + KG, kx:kx + W],
                                          start=(kx + nxt == 0), stop=(kx + nxt == 3))
                        last.then_inc(a_conv, 1)

                pe.wait_ge(s_act, 3)
                centre_image(0, 0)

                def image(b, i, r, left):
                    if not isinstance(b, int) or left:
                        centre_image(b + 1, i + 1)
                    conv_image(b, i)

                body_of_images(pe, image)

                for n in range(2):
                    pe.wait_ge(a_stats, B + 1 + 3 * n)
                    mm(ps[:, 0, n:n + 1], halves[:], bn[:, 4 + n:5 + n], start=True, stop=True).then_inc(s_pe, 1)

                pe.wait_ge(s_dve, DVE_TMP)
                mm(ps[:, 2], ones64[:], tmp[:], start=True, stop=True).then_inc(s_pe, 1)

                def layer1(k, n):
                    unit, g, q = UNITS * k + n, n // PAIRS, n % PAIRS
                    if q == 0:
                        pe.wait_ge(slo_done, G * k + g + 1 + G)
                    for par in range(2):
                        pe.wait_ge(hlo_done[par], unit + 1)
                        at = ps[:, 2 * (n % 2) + par, 0:NG]
                        mm(at, w1hi[:, P * q:P * q + P], stack[:, par, g, :], start=True, stop=False)
                        mm(at, w1lo[:, P * q:P * q + P], stack[:, par, g, :], start=False, stop=True).then_inc(z1_full[par], 1)

                def layer2(k, n):
                    unit, q = UNITS * k + n, n % PAIRS
                    for par in range(2):
                        pe.wait_ge(hlo_done[par], unit + 1 + RING2)
                        pe.wait_ge((v0_done, relu1_done)[par], unit + 1)
                        at = ps[:, 4 + par, 0:NG]
                        mm(at, w2hi[:, q, :], hhi[:, n % 2, par, :], start=True, stop=False)
                        mm(at, w2lo[:, q, :], hhi[:, n % 2, par, :], start=False, stop=False)
                        mm(at, w2hi[:, q, :], hlo[:, n % 2, par, :], start=False, stop=True).then_inc(z2_full[par], 1)

                def layer3(k, n):
                    unit, g, q = UNITS * k + n, n // PAIRS, n % PAIRS
                    pe.wait_ge(v0_done, unit + 2)
                    pe.wait_ge(v1_done, unit + 1)
                    if q == 0:
                        pe.wait_ge(out_done, G * k + g + 1)
                    for par in range(2):
                        last = mm(ps[64 * par:64 * par + 64, 6, 0:NG], wo[:, q, :], v[:, n % 2, par, :],
                                  start=(q == 0), stop=(q == PAIRS - 1))
                    last.then_inc(l3_done, 1)

                def prep(q, h):
                    if h in AT_CENTRE:
                        g = AT_CENTRE.index(h)
                        pe.wait_ge(pl_done, G * q + g + 1)
                        pe.wait_ge(xc_done, G * q + g + 1)
                        if g == 0:
                            pe.wait_ge(g_done, q + 1)
                        mm(misc[:, 0:NG], centre[:], ph[:, g % 2, :], start=True, stop=False)
                        mm(misc[:, 0:NG], centre[:], pl[:, g % 2, :], start=False, stop=True).then_inc(centre_done, 1)
                    if h == AT_VAR:
                        pe.wait_ge(xc_done, G * q + G + 1)
                        for g in range(G):
                            last = mm(misc[32 * g:32 * g + 32, 0:NG], var_ones[:], t[:, g, :], start=True, stop=True)
                        last.then_inc(var_done, 1)
                    if h in AT_SPREAD:
                        g = AT_SPREAD.index(h)
                        if g == 0:
                            pe.wait_ge(rs_done, q + 1)
                        else:
                            pe.wait_ge(rb_done, G * q + g)
                        r = slice(32 * g, 32 * g + 32)
                        mm(misc[:, 0:NG], spread[r, :], rhi[r, :], start=True, stop=False)
                        mm(misc[:, 0:NG], spread[r, :], rlo[r, :], start=False, stop=True).then_inc(rb_full, 1)
                    if h == AT_LOGITS:
                        pe.wait_ge(feat_done, q + 1)
                        pe.wait_ge(rb_done, G * q + G)
                        mm(misc[0:W, 0:2 * E], feat[:], wr[:].rearrange("p a e -> p (a e)"), start=True, stop=True).then_inc(logits_done, 1)
                    if h == AT_WB:
                        pe.wait_ge(gate_done, q + 1)
                        for pair in range(PAIRS):
                            for par in range(2):
                                at = (2 * pair + par) * W
                                for half in range(2):
                                    e = 2 * pair + half
                                    mm(misc[64 * half:64 * half + 64, at:at + W], gate_w[:, par, e:e + 1].broadcast_to([P, C]),
                                       ident[:, 0:W], start=True, stop=True)
                        mm(misc[0:2 * E, NG:NG + W], gate_w[:].rearrange("p a e -> p (a e)"), ident[:, 0:W],
                           start=True, stop=True).then_inc(wb_full, 1)
                    if h == AT_G:
                        pe.wait_ge(wb_done, q + 1)
                        mm(misc[:, 0:W], expert_const[:], wT[:], start=True, stop=True).then_inc(g_full, 1)

                def chunk(k, s, j, last):
                    for n in range(UNITS):
                        if 1 <= n < UNITS - 1:
                            layer1(k, n + 1)
                        elif n and not last:
                            layer1(k + 1, 0)
                        layer2(k, n)
                        if not last:
                            prep(k + 1, 2 * n)
                        if n:
                            layer3(k, n - 1)
                        if not last:
                            prep(k + 1, 2 * n + 1)
                    if not last:
                        layer1(k + 1, 1)
                    layer3(k, UNITS - 1)

                for h in range(AT_LOGITS):
                    prep(0, h)
                pe.wait_ge(s_dve, DVE_C2SEL)
                for q in range(PAIRS):
                    last = mm(ps[0:2 * E, 3, 0:C], c2sel[:, q, :], wo[:, q, :], start=(q == 0), stop=(q == PAIRS - 1))
                last.then_inc(s_pe, 1)
                pe.wait_ge(s_dve, DVE_ALL)
                for h in range(AT_LOGITS, 2 * UNITS):
                    prep(0, h)
                layer1(0, 0)
                layer1(0, 1)
                body_of_chunks(pe, chunk)

            @block.scalar
            def _(act):
                for s, n in ((a_signed, RINGA), (a_kept, RINGA), (relu1_done, 1), (xc_done, 1), (g_done, 1)):
                    act.sem_inc(s, n)
                A = nc.scalar.activation
                act.wait_ge(s_dve, 6)
                A(bn[:, 8:9], bn[:, 7:8], ACT.Sqrt, scale=1.0 / (C * TAPS - 1)).then_inc(s_act, 1)
                A(cwsign[:, :, 1:4, :], cwt[0:64].rearrange("p ci ky kx -> p kx ky ci"), ACT.Sign).then_inc(s_act, 1)
                act.wait_ge(s_pe, 1)
                A(convw[:, 0:2].rearrange("p k a m -> p (k a m)"), ps[:, 0, :], ACT.Copy)
                A(convw[:, 2].rearrange("p a m -> p (a m)"), ps[:, 1, 0:256], ACT.Copy).then_inc(s_act, 1)
                def sign_image(b, i):
                    act.wait_ge(a_conv, GA * b + GA)
                    for g in range(GA):
                        lo, hi = slot_group(g)
                        act.wait_ge(a_centred, GA * b + g + 1)
                        A(sgn[:, i % 2, lo:hi, 1:W + 1], ps[:, g, 0:(hi - lo) * W].rearrange("p (k w) -> p k w", w=W),
                          ACT.Sign).then_inc(a_signed, 1)

                def keep_image(b):
                    for g in range(GA):
                        act.wait_ge(a_conv, GA * b + g + 1 + RINGS)
                        yb = y[:, KG * g:KG * g + KG, b, :] if isinstance(b, int) else \
                            y[:, KG * g:KG * g + KG, bass.ds(b, 1), :].rearrange("p k o w -> p (k o) w")
                        A(yb, ps[:, GA + g, 0:KG * W].rearrange("p (k w) -> p k w", w=W), ACT.Copy).then_inc(a_kept, 1)

                act.wait_ge(s_zero, 1)
                sign_image(0, 0)

                def image(b, i, r, left):
                    if not isinstance(b, int) or left:
                        sign_image(b + 1, i + 1)
                    keep_image(b)

                def fold_roots():
                    act.wait_ge(s_dve, DVE_VAR)
                    A(rows[:, 1, :], rows[:, 1, :], ACT.Sqrt)
                    A(rows[:, 6, :], rows[:, 6, :], ACT.Sqrt)
                    A(cols[:, 1, :], cols[:, 1, :], ACT.Sqrt).then_inc(s_act, 1)

                body_of_images(act, image, fold_roots)
                act.wait_ge(a_stats, B + 5)
                A(bn[:, 11:12], bn[:, 10:11], ACT.Sqrt).then_inc(s_act, 1)

                def relu_hi(k, n):
                    unit = UNITS * k + n
                    for par in range(2):
                        act.wait_ge(z1_full[par], unit + 1)
                        act.wait_ge(z2_full[par], unit + 1)
                        A(hhi[:, n % 2, par, :], ps[:, 2 * (n % 2) + par, 0:NG], ACT.Relu).then_inc(hhi_done[par], 1)

                def relu1(k, n):
                    unit = UNITS * k + n
                    act.wait_ge(z2_full[1], unit + 1 + RING2)
                    act.wait_ge(l3_done, unit + 1)
                    A(v[:, n % 2, 1, :], ps[:, 5, 0:NG], ACT.Relu, bias=bias2[:, n % PAIRS:n % PAIRS + 1]).then_inc(relu1_done, 1)

                def prep(q, s, h):
                    if h in AT_T:
                        g = AT_T.index(h)
                        act.wait_ge(u_done, G * q + g + 1)
                        yq = y[:, q, BG * g:BG * g + BG, :] if isinstance(q, int) else \
                            y[:, bass.ds(q, 1), BG * g:BG * g + BG, :].rearrange("p o b w -> p (o b) w")
                        A(t[:, g].rearrange("p (b w) -> p b w", w=W), yq, ACT.Identity, bias=OFFSET, scale=SCALE).then_inc(t_done, 1)
                    if h in AT_SPLIT:
                        g = AT_SPLIT.index(h)
                        act.wait_ge(x1_done, G * q + g + 1 + RING2)
                        act.wait_ge(centre_done, G * q + g + 1)
                        A(ph[:, g % 2, :], o[:, s, BG * g:BG * g + BG, :].rearrange("p b w -> p (b w)"), ACT.Copy).then_inc(ph_done, 1)
                    if h - 1 in AT_CENTRE:
                        g = AT_CENTRE.index(h - 1)
                        act.wait_ge(centre_done, G * q + g + 1 + RING2)
                        act.wait_ge(slo_done, G * q + g + 1)
                        A(t[:, g], misc[:, 0:NG], ACT.Square)
                        A(xc[:, g, :], misc[:, 0:NG], ACT.Copy).then_inc(xc_done, 1)
                    if h == AT_VAR + 1:
                        act.wait_ge(var_done, q + 1)
                        A(rs[:], misc[:, 0:NG], ACT.Sqrt, bias=LN_EPS).then_inc(sqrt_done, 1)
                    if h in AT_SPREAD:
                        g = AT_SPREAD.index(h)
                        act.wait_ge(rb_full, G * q + g + 1)
                        A(t[:, g], misc[:, 0:NG], ACT.Copy).then_inc(rb_done, 1)
                    if h in AT_STACK:
                        g = AT_STACK.index(h)
                        act.wait_ge(u_done, G * q + g + 1 + G)
                        for par in range(2):
                            half = slice(64 * par, 64 * par + 64)
                            A(stack[half, par, g, :], xc[half, g, :], ACT.Copy, bias=SHIFT).then_inc(shi_done, 1)
                    if h == AT_EXP:
                        act.wait_ge(gate_sub, q + 1)
                        A(gate_e[:], gate[:], ACT.Exp).then_inc(gate_exp, 1)
                    if h == AT_WBC:
                        act.wait_ge(wb_full, q + 1)
                        A(wT[:], misc[0:2 * E, NG:NG + W], ACT.Copy)
                        A(wb[:, s].rearrange("p a b w -> p (a b w)"), misc[:, 0:NG], ACT.Copy).then_inc(wb_done, 1)
                    if h == AT_GC:
                        act.wait_ge(g_full, q + 1)
                        A(gconst[:, s, :], misc[:, 0:W], ACT.Copy).then_inc(g_done, 1)

                def chunk(k, s, j, last):
                    for n in range(UNITS):
                        if n + 1 < UNITS:
                            relu_hi(k, n + 1)
                        elif not last:
                            relu_hi(k + 1, 0)
                        if not last:
                            prep(k + 1, 1 - s, 2 * n)
                        relu1(k, n)
                        if not last:
                            prep(k + 1, 1 - s, 2 * n + 1)

                act.wait_ge(s_bn, 1)
                for h in range(2 * UNITS):
                    prep(0, 0, h)
                relu_hi(0, 0)
                body_of_chunks(act, chunk)

            @block.vector
            def _(dve):
                V = nc.vector
                for s, n in ((slo_done, G), (hlo_done[0], RING2), (hlo_done[1], RING2), (v0_done, 1), (out_done, 1)):
                    dve.sem_inc(s, n)
                V.memset(xa[:, :, 0:1, :], 0.0)
                V.memset(xa[:, :, RP:SLOTS, :], 0.0)
                V.memset(sgn[:], 0.0).then_inc(s_zero, 1)
                V.memset(w2raw[:], 0.0)
                V.memset(wr[:], 0.0)
                V.memset(expert_const[:], 0.0)
                V.memset(c2sel[:], 0.0)
                V.memset(cwsign[:], 0.0).then_inc(s_zero, 1)

                count = [0]

                def step(ins):
                    count[0] += 1
                    ins.then_inc(s_dve, 1)
                    dve.wait_ge(s_dve, count[0])

                dve.wait_ge(s_cw, 16 * N_CW)
                dve.wait_ge(s_zero, 2)
                cflat = cwt[:].rearrange("p a b c -> p (a b c)")
                step(V.tensor_reduce(bn[:, 3:4], cflat, AX.X, ALU.add))
                step(V.tensor_scalar(bn[:, 3:4], bn[:, 3:4], 1.0 / (C * TAPS), None, ALU.mult))
                step(V.tensor_scalar(cflat, cflat, bn[:, 3:4], None, ALU.subtract))
                step(V.tensor_tensor(cwa[:], cflat, cflat, ALU.mult))
                step(V.tensor_reduce(bn[:, 7:8], cwa[:], AX.X, ALU.add))
                dve.wait_ge(s_const, 9)
                step(V.tensor_copy(identb[:], ident[0:64, 0:64]))
                step(V.scalar_tensor_tensor(out=cwa[:], in0=cflat, scalar=-1.0, in1=cflat, op0=ALU.mult, op1=ALU.max))
                step(V.tensor_reduce(bn[:, 9:10], cwa[:], AX.X, ALU.add))

                dve.wait_ge(s_act, 1)
                step(V.reciprocal(SW, bn[:, 8:9]))
                step(V.tensor_scalar(bn[:, 9:10], bn[:, 9:10], SW, SQRT2 / (C * TAPS), ALU.mult, ALU.mult))
                step(V.tensor_scalar(SW.bitcast(I32), bn[:, 9:10].bitcast(I32), EXP_MASK, None, ALU.bitwise_and))

                V.tensor_tensor(centre[:], ident[:], ones64[:], ALU.subtract)
                dve.wait_ge(s_const, 15)
                step(V.tensor_copy(spread[:], tmp[:, 0:P]))

                r1 = lambda i: rows[:, i, :]

                def fold_scales():
                    dve.wait_ge(s_ffn, 16 * N_FFN)
                    V.tensor_scalar(r1(1), r1(1), BNF_EPS, None, ALU.add)
                    V.tensor_scalar(r1(6), r1(6), BNF_EPS, None, ALU.add)
                    V.tensor_tensor(r1(2), r1(2), r1(3), ALU.subtract)
                    V.tensor_tensor(cols[:, 2, :], cols[:, 2, :], cols[:, 3, :], ALU.subtract)
                    V.tensor_scalar(wr[:], wr[:], 1.0 / B, None, ALU.mult)
                    step(V.tensor_scalar(cols[:, 1, :], cols[:, 1, :], BNF_EPS, None, ALU.add))
                    dve.wait_ge(s_act, 4)
                    V.reciprocal(r1(6), r1(6))
                    V.reciprocal(cols[:, 1, :], cols[:, 1, :])
                    step(V.reciprocal(r1(1), r1(1)))
                    V.tensor_tensor(r1(6), r1(6), r1(5), ALU.mult)
                    V.tensor_tensor(cols[:, 1, :], cols[:, 1, :], cols[:, 0, :], ALU.mult)
                    step(V.tensor_tensor(r1(1), r1(1), r1(0), ALU.mult))
                    step(V.tensor_tensor(tmp[:], wraw[:].rearrange("p e h -> p (e h)"), r1(1), ALU.mult))
                    step(V.tensor_tensor(r1(2), r1(2), r1(1), ALU.mult))
                    step(V.tensor_tensor(r1(2), r1(2), r1(4), ALU.add))

                def fold_parts():
                    dve.wait_ge(s_pe, 4)
                    step(V.scalar_tensor_tensor(out=r1(2), in0=r1(2), scalar=1.0 / (C * SHIFT), in1=ps[:, 2],
                                                op0=ALU.mult, op1=ALU.subtract))
                    step(V.tensor_tensor(tmp[:], tmp[:], r1(2), ALU.add))
                    step(V.tensor_copy(w1hi[:], tmp[:]))
                    step(V.tensor_tensor(w1lo[:], tmp[:], w1hi[:].bitcast(F32), ALU.subtract))
                    dve.wait_ge(s_w2, 16 * N_W2)
                    w2f, w2h, w2l = (a[:].rearrange("p q m -> p (q m)") for a in (w2raw, w2hi, w2lo))
                    step(V.tensor_tensor(w2f, w2f, r1(6), ALU.mult))
                    step(V.tensor_copy(w2h, w2f))
                    step(V.tensor_tensor(w2l, w2f, w2h.bitcast(F32), ALU.subtract))
                    step(V.tensor_tensor(cols[:, 2, :], cols[:, 2, :], cols[:, 1, :], ALU.mult))
                    step(V.tensor_tensor(bias2[:], cols[:, 2, :], cols[:, 4, :], ALU.add))
                    step(V.tensor_scalar(negb2[:], bias2[:], -1.0, None, ALU.mult))
                    for q in range(PAIRS):
                        V.tensor_copy(c2sel[0:64, q, 2 * q:2 * q + 1], bias2[0:64, q:q + 1])
                        last = V.tensor_copy(c2sel[64:128, q, 2 * q + 1:2 * q + 2], bias2[64:128, q:q + 1])
                    step(last)

                def split(b, i, r):
                    s4 = i % XRING
                    dve.wait_ge(s_xa[s4], 32 * (r + i // XRING) + 32)
                    if not (isinstance(b, int) and b < 2):
                        dve.wait_ge(a_centred, GA * b - GA)
                    V.tensor_copy(xhi[:, i % 2], xa[:, s4]).then_inc(a_hi, 1)
                    dve.wait_ge(a_hi, b + 1)
                    V.tensor_tensor(xlo[:, i % 2], xa[:, s4], xhi[:, i % 2].bitcast(F32), ALU.subtract).then_inc(a_split, 1)

                def image_stats(b):
                    for g in range(GA):
                        dve.wait_ge(a_kept, GA * b + g + 1 + RINGA)
                        k = slice(KG * g, KG * g + KG)
                        if isinstance(b, int):
                            yb, sb_ = y[:, k, b, :], stats[:, b, g, :]
                        else:
                            yb = y[:, k, bass.ds(b, 1), :].rearrange("p k o w -> p (k o) w")
                            sb_ = stats[:, bass.ds(b, 1), g, :].rearrange("p o s -> p (o s)")
                        last = V.bn_stats(sb_, yb)
                    last.then_inc(a_stats, 1)

                split(0, 0, 0)
                split(1, 1, 0)

                def image(b, i, r, left):
                    if not isinstance(b, int) or left >= 2:
                        split(b + 2, i + 2, r)
                    image_stats(b)

                body_of_images(dve, image, fold_scales)

                mean, var = bn[:, 12:13], bn[:, 13:14]
                dve.wait_ge(a_stats, B)
                V.bn_aggr(bn[:, 4:6], stats[:].rearrange("p b g s -> p (b g s)")).then_inc(a_stats, 1)
                dve.wait_ge(s_pe, 2)
                V.tensor_copy(mean, ps[:, 0, 0:1]).then_inc(a_stats, 1)
                dve.wait_ge(a_stats, B + 2)
                V.tensor_tensor(bn[:, 14:15], bn[:, 4:5], mean, ALU.subtract).then_inc(a_stats, 1)
                dve.wait_ge(a_stats, B + 3)
                V.scalar_tensor_tensor(out=bn[:, 5:6], in0=bn[:, 14:15], scalar=bn[:, 14:15], in1=bn[:, 5:6],
                                       op0=ALU.mult, op1=ALU.add).then_inc(a_stats, 1)
                dve.wait_ge(s_pe, 3)
                V.tensor_scalar(bn[:, 13:14], ps[:, 0, 1:2], SW, None, ALU.mult).then_inc(d_bn, 1)
                dve.wait_ge(d_bn, 1)
                V.tensor_scalar(bn[:, 10:11], var, SW, BN1_EPS, ALU.mult, ALU.add).then_inc(a_stats, 1)
                dve.wait_ge(s_act, 5)
                V.reciprocal(bn[:, 15:16], bn[:, 11:12]).then_inc(d_bn, 1)
                dve.wait_ge(d_bn, 2)
                V.tensor_scalar(bn[:, 14:15], bn[:, 15:16], SW, None, ALU.mult).then_inc(d_bn, 1)
                dve.wait_ge(d_bn, 3)
                V.tensor_scalar(SCALE, bn[:, 14:15], gb[:, 0:1], None, ALU.mult).then_inc(d_bn, 1)
                dve.wait_ge(d_bn, 4)
                V.tensor_scalar(bn[:, 14:15], mean, SCALE, None, ALU.mult).then_inc(d_bn, 1)
                dve.wait_ge(d_bn, 5)
                V.tensor_tensor(OFFSET, gb[:, 1:2], bn[:, 14:15], ALU.subtract).then_inc(s_bn, 1)

                def relu_lo(k, n):
                    unit = UNITS * k + n
                    for par in range(2):
                        dve.wait_ge(hhi_done[par], unit + 1)
                        V.scalar_tensor_tensor(out=hlo[:, n % 2, par, :], in0=ps[:, 2 * (n % 2) + par, 0:NG], scalar=0.0,
                                               in1=hhi[:, n % 2, par, :].bitcast(F32), op0=ALU.max, op1=ALU.subtract).then_inc(hlo_done[par], 1)

                def v0(k, s, n):
                    unit, q = UNITS * k + n, n % PAIRS
                    if n == 0:
                        dve.wait_ge(wb_done, k + 1)
                    dve.wait_ge(z2_full[0], unit + 1 + RING2)
                    dve.wait_ge(l3_done, unit + 1)
                    V.scalar_tensor_tensor(out=v[:, n % 2, 0, :].rearrange("p (b w) -> p b w", w=W),
                                           in0=ps[:, 4, 0:NG].rearrange("p (b w) -> p b w", w=W), scalar=negb2[:, q:q + 1],
                                           in1=wb[:, s, q, 0:1, :].broadcast_to([P, BG, W]),
                                           op0=ALU.max, op1=ALU.mult).then_inc(v0_done, 1)

                def add_out(k, s, g):
                    dve.wait_ge(l3_done, UNITS * k + PAIRS * g + PAIRS + RING2)
                    dve.wait_ge(x1g_done, G * k + g + 1)
                    og = o[:, s, BG * g:BG * g + BG, :].rearrange("p b w -> p (b w)")
                    V.tensor_tensor(og, ps[:, 6, 0:NG], og, ALU.add).then_inc(out_done, 1)

                GATE_STEPS, RS_STEPS = 4, 5

                def prep(q, s, h):
                    if h in AT_T:
                        g = AT_T.index(h)
                        dve.wait_ge(t_done, G * q + g + 1)
                        V.tensor_scalar(t[:, g, :], t[:, g, :], 1.0, -1.0, ALU.min, ALU.max).then_inc(clip_done, 1)
                    if h in AT_SPLIT:
                        g = AT_SPLIT.index(h)
                        dve.wait_ge(ph_done, G * q + g + 1)
                        V.tensor_tensor(pl[:, g % 2, :], o[:, s, BG * g:BG * g + BG, :].rearrange("p b w -> p (b w)"),
                                        ph[:, g % 2, :].bitcast(F32), ALU.subtract).then_inc(pl_done, 1)
                    if h in AT_INV:
                        i = AT_INV.index(h)
                        if i == 0:
                            dve.wait_ge(sqrt_done, q + 1)
                        cut = slice(i * NG // 4, (i + 1) * NG // 4)
                        V.reciprocal(rs[:, cut], rs[:, cut]).then_inc(d_rs, 1)
                        if i == 3:
                            dve.wait_ge(d_rs, RS_STEPS * q + 4)
                            V.tensor_copy(rhi[:], rs[:]).then_inc(d_rs, 1)
                            dve.wait_ge(d_rs, RS_STEPS * q + 5)
                            V.tensor_tensor(rlo[:], rs[:], rhi[:].bitcast(F32), ALU.subtract).then_inc(rs_done, 1)
                    if h in AT_FEAT:
                        g = AT_FEAT.index(h)
                        dve.wait_ge(u_done, G * q + g + 1 + G)
                        V.tensor_reduce(feat4[:, g, :], xc[:, g, :].rearrange("p (b w) -> p w b", w=W), AX.X, ALU.add).then_inc(d_feat, 1)
                        if g == G - 1:
                            dve.wait_ge(d_feat, G * q + G)
                            V.tensor_reduce(feat[:], feat4[:].rearrange("p g w -> p w g"), AX.X, ALU.add).then_inc(feat_done, 1)
                    if h in AT_STACK:
                        g = AT_STACK.index(h)
                        for par in range(2):
                            half = slice(64 * par, 64 * par + 64)
                            other = slice(64 - 64 * par, 128 - 64 * par)
                            dve.wait_ge(shi_done, 2 * (G * q + g) + par + 1)
                            last = V.scalar_tensor_tensor(out=stack[other, par, g, :], in0=xc[half, g, :], scalar=SHIFT,
                                                          in1=stack[half, par, g, :].bitcast(F32), op0=ALU.add, op1=ALU.subtract)
                        last.then_inc(slo_done, 1)
                    if h == AT_LOGITS:
                        dve.wait_ge(logits_done, q + 1)
                        V.tensor_tensor(gate[:].rearrange("p a e -> p (a e)"), misc[0:W, 0:2 * E], brb[:].rearrange("p a e -> p (a e)"), ALU.add).then_inc(d_gate, 1)
                        dve.wait_ge(d_gate, GATE_STEPS * q + 1)
                        V.tensor_reduce(gate_s[:, :, 0:1], gate[:], AX.X, ALU.max).then_inc(d_gate, 1)
                        dve.wait_ge(d_gate, GATE_STEPS * q + 2)
                        V.tensor_tensor(gate[:], gate[:], gate_s[:, :, 0:1].broadcast_to([W, 2, E]), ALU.subtract).then_inc(gate_sub, 1)
                    if h == AT_GATE:
                        dve.wait_ge(gate_exp, q + 1)
                        V.tensor_reduce(gate_s[:, :, 0:1], gate_e[:], AX.X, ALU.add).then_inc(d_gate, 1)
                        dve.wait_ge(d_gate, GATE_STEPS * q + 3)
                        V.reciprocal(gate_s[:, :, 1:2], gate_s[:, :, 0:1]).then_inc(d_gate, 1)
                        dve.wait_ge(d_gate, GATE_STEPS * q + 4)
                        V.tensor_tensor(gate_w[0:W], gate_e[:], gate_s[:, :, 1:2].broadcast_to([W, 2, E]), ALU.mult).then_inc(gate_done, 1)

                def chunk(k, s, j, last):
                    for n in range(UNITS):
                        if n + 1 < UNITS:
                            relu_lo(k, n + 1)
                        elif not last:
                            relu_lo(k + 1, 0)
                        if not last:
                            prep(k + 1, 1 - s, 2 * n)
                        if n % PAIRS == 0 and n:
                            add_out(k, s, n // PAIRS - 1)
                        v0(k, s, n)
                        if not last:
                            prep(k + 1, 1 - s, 2 * n + 1)
                    add_out(k, s, G - 1)

                V.memset(gate_w[:], 0.0).then_inc(d_bn, 1)
                fold_parts()
                dve.wait_ge(d_bn, 6)
                for h in range(AT_LOGITS):
                    prep(0, 0, h)
                dve.wait_ge(s_pe, 5)
                step(V.tensor_tensor(expert_const[:, 0:C], expert_const[:, 0:C], ps[0:2 * E, 3, 0:C], ALU.add))
                for h in range(AT_LOGITS, 2 * UNITS):
                    prep(0, 0, h)
                relu_lo(0, 0)
                body_of_chunks(dve, chunk)


_INS = ["x", "L0_conv_weight", "L0_conv_gamma", "L0_conv_beta", "L0_ffn_Wr", "L0_ffn_br", "L0_ffn_W1", "L0_ffn_b1",
        "L0_ffn_g1", "L0_ffn_be1", "L0_ffn_m1", "L0_ffn_v1", "L0_ffn_W2", "L0_ffn_b2", "L0_ffn_g2", "L0_ffn_be2",
        "L0_ffn_m2", "L0_ffn_v2", "L0_ffn_Wo", "L0_ffn_bo"]


def kernel(**inputs):
    import numpy as _np
    import concourse.bacc as _bacc
    from concourse.bass_utils import run_bass_kernel_spmd as _run

    nc = _bacc.Bacc("TRN2", target_bir_lowering=False, num_devices=1)
    arrays, args = {}, []
    for name in _INS:
        a = _np.ascontiguousarray(inputs[name])
        arrays[f"in_{name}"] = a
        args.append(nc.dram_tensor(f"in_{name}", a.shape, mybir.dt.from_np(a.dtype), kind="ExternalInput").ap())
    args.append(nc.dram_tensor("out", (B, C, H, W), F32, kind="ExternalOutput").ap())
    metaformer_kernel(nc, *args)
    r = _run(nc, [arrays], core_ids=[0])
    return r.results[0]["out"]
```

```python
from contextlib import ExitStack

import concourse.bass as bass
from concourse import mybir

F32 = mybir.dt.float32
F32R = mybir.dt.float32r
F16 = mybir.dt.float16
BF16 = mybir.dt.bfloat16
I32 = mybir.dt.int32
ALU = mybir.AluOpType
ACT = mybir.ActivationFunctionType
AX = mybir.AxisListType

P = 128
B, C, H, W = 32, 64, 56, 56
E = 8
PAIRS = E // 2
RP = H // 2
SLOTS = RP + 1
TAPS = 9
GA = 4
KG = RP // GA
XRING = 4
G = 4
BG = B // G
NG = BG * W
UNITS = G * PAIRS
LN_EPS, BN1_EPS, BNF_EPS = 1e-5, 1e-5, 1e-3
SHIFT = 0.125
EXP_MASK = 0x7F800000
SQRT2 = 2.0 ** 0.5


class Schedule:

    def __init__(self, t, split, low_by_vector, centre, var, inv, parts, spread, norm, norm_by_vector, feat, stack,
                 logits, exp, gate, wb, const):
        self.t, self.split, self.low_by_vector, self.centre = t, split, low_by_vector, centre
        self.var, self.inv, self.spread, self.norm = var, inv, spread, norm
        self.norm_by_vector, self.feat, self.parts = norm_by_vector, feat, parts
        self.stack, self.logits, self.exp, self.gate, self.wb, self.const = stack, logits, exp, gate, wb, const


def slot_group(i):
    return (0 if i == 0 else KG * i + 1), KG * (i + 1) + 1


def metaformer_kernel(nc, x, cw, gamma, beta, Wr, br, W1, b1, g1, be1, m1, v1, W2, b2, g2, be2, m2, v2, Wo, bo, out):
    with ExitStack() as ctx:
        def sb(name, shape, dt, to=ctx):
            return to.enter_context(nc.sbuf_tensor(name, shape, dt))

        def sem(name):
            return ctx.enter_context(nc.semaphore(name))

        XIN_OVER = -(-B // SLOTS)
        y = sb("y", [P, RP, B, W], F16)
        ident = sb("ident", [P, P], F32)
        ones64 = sb("ones64", [P, P], F32)
        centre = sb("centre", [P, P], F32R)
        var_ones = sb("var_ones", [P, 32], F32)
        spread = sb("spread", [P, P], F32R)
        low_rows = sb("low_rows", [P, 1], F32)
        low_pattern = sb("low_pattern", [P, G, 2], F32)
        halves = sb("halves", [P, P], F32)
        convw = sb("convw", [P, 3, 2, P], BF16)
        w1hi = sb("w1hi", [P, E * C], F32R)
        w1lo = sb("w1lo", [P, E * C], F32R)
        w2hi = sb("w2hi", [P, PAIRS, P], F32R)
        w2lo = sb("w2lo", [P, PAIRS, P], F32R)
        wo = sb("wo", [P, PAIRS, C], F32)
        wr = sb("wr", [P, 2, E], F32)
        brb = sb("brb", [W, 2, E], F32)
        bias2 = sb("bias2", [P, PAIRS], F32)
        negb2 = sb("negb2", [P, PAIRS], F32)
        expert_const = sb("expert_const", [2 * E, P], F32)
        bn = sb("bn", [P, 16], F32)
        SCALE, OFFSET, SW = bn[:, 0:1], bn[:, 1:2], bn[:, 2:3]
        gb = sb("gb", [P, 2], F32)

        fold = ExitStack()
        rows = sb("rows", [P, 7, E * C], F32, fold)
        cols = sb("cols", [P, 6, PAIRS], F32, fold)
        wraw = sb("wraw", [P, E, C], F32, fold)
        w2raw = sb("w2raw", [P, PAIRS, P], F32, fold)
        c2sel = sb("c2sel", [P, PAIRS, 2 * E], F32, fold)
        tmp = sb("tmp", [P, E * C], F32, fold)
        fold.close()
        hhi = sb("hhi", [P, 2, 2, NG], F32R)
        hlo = sb("hlo", [P, 2, 2, NG], F32R)
        v = sb("v", [P, 2, 2, NG], F32)

        early = ExitStack()
        xa = sb("xa", [P, XRING, SLOTS, W], F32, early)
        xhi = sb("xhi", [P, 2, SLOTS, W], F32R, early)
        xlo = sb("xlo", [P, 2, SLOTS, W], F32R, early)
        sgn = sb("sgn", [P, 2, SLOTS, W + 2], BF16, early)
        stats = sb("stats", [P, B, GA, 6], F32, early)
        cwt = sb("cwt", [P, C, 3, 3], F32, early)
        cwa = sb("cwa", [P, C * TAPS], F32, early)
        cwsign = sb("cwsign", [C, 3, 5, C], BF16, early)
        identb = sb("identb", [C, C], BF16, early)
        early.close()

        xin = sb("xin", [P, B, W], F32)
        o = sb("o", [P, 2, B, W], F32)
        t = sb("t", [P, G, NG], F32)
        ph = sb("ph", [P, 2, NG], F32R)
        pl = sb("pl", [P, 2, NG], F32R)
        xc = sb("xc", [P, G, NG], F32)
        rs = sb("rs", [P, NG], F32)
        sq = sb("sq", [P, NG], F32)
        rhi = sb("rhi", [P, NG], F32R)
        rparts = sb("rparts", [P, NG], F32R)
        feat4 = sb("feat4", [P, G, W], F32)
        feat = sb("feat", [P, W], F32)
        stack = sb("stack", [P, 2, G, NG], F32R)
        gate = sb("gate", [W, 2, E], F32)
        gate_e = sb("gate_e", [W, 2, E], F32)
        gate_w = sb("gate_w", [P, 2, E], F32)
        gate_s = sb("gate_s", [W, 2, 2], F32)
        wT = sb("wT", [2 * E, W], F32)
        wb = sb("wb", [P, 2, PAIRS, 2, W], F32)
        gconst = sb("gconst", [P, 2, W], F32)

        ps = ctx.enter_context(nc.psum_tensor("ps", [P, 8, 512], F32))
        misc = ps[:, 7]

        s_cw = sem("s_cw")
        s_ffn = sem("s_ffn")
        s_w2 = sem("s_w2")
        s_const = sem("s_const")
        s_zero = sem("s_zero")
        s_dve = sem("s_dve")
        f_pool = sem("f_pool")
        f_act = sem("f_act")
        f_dve = sem("f_dve")
        s_act = sem("s_act")
        s_pe = sem("s_pe")
        s_xa = [sem(f"s_xa{i}") for i in range(XRING)]
        a_hi = sem("a_hi")
        a_split = sem("a_split")
        a_centred = sem("a_centred")
        a_signed = sem("a_signed")
        a_conv = sem("a_conv")
        a_kept = sem("a_kept")
        a_stats = sem("a_stats")
        d_bn = sem("d_bn")
        s_bn = sem("s_bn")
        x_loaded = sem("x_loaded")
        t_done = sem("t_done")
        clip_done = sem("clip_done")
        x1_done = sem("x1_done")
        ph_done = sem("ph_done")
        pl_done = [sem(f"pl_done{g}") for g in range(G)]
        centre_done = sem("centre_done")
        xc_done = sem("xc_done")
        var_done = sem("var_done")
        root_steps = sem("root_steps")
        root_done = sem("root_done")
        rs_done = sem("rs_done")
        d_rs = sem("d_rs")
        rb_full = sem("rb_full")
        rb_done = [sem(f"rb_done{g}") for g in range(G)]
        u_done = [sem(f"u_done{g}") for g in range(G)]
        shi_done = sem("shi_done")
        slo_done = sem("slo_done")
        feat_done = sem("feat_done")
        logits_done = sem("logits_done")
        gate_sub = sem("gate_sub")
        gate_exp = sem("gate_exp")
        gate_done = sem("gate_done")
        wb_full = sem("wb_full")
        wb_done = sem("wb_done")
        g_full = sem("g_full")
        g_done = sem("g_done")
        x1g_done = sem("x1g_done")
        d_feat = sem("d_feat")
        d_gate = sem("d_gate")
        z1_full = [sem(f"z1_full{i}") for i in range(2)]
        hhi_done = [sem(f"hhi_done{i}") for i in range(2)]
        hlo_done = [sem(f"hlo_done{i}") for i in range(2)]
        z2_full = [sem(f"z2_full{i}") for i in range(2)]
        v0_done = sem("v0_done")
        relu1_done = sem("relu1_done")
        v1_done = sem("v1_done")
        l3_done = sem("l3_done")
        out_done = sem("out_done")
        stored = [[sem(f"stored{i}_{g}") for g in range(G)] for i in range(2)]

        RING2, RINGA, RINGS = 2, GA, 2 * GA

        x_pairs = x.rearrange("b c (k two) w -> b c k two w", two=2)
        N_CW, N_W2, N_FFN = 4, 4, 21
        FOLD_VAR = 4
        FOLD_TMP = 23
        FOLD_ALL = 36
        FOLD_DVE = 7
        DVE_SPREAD = 12

        HALVES = 2 * UNITS
        STEADY = Schedule(
            t=(1, 3, 6, 9),
            split=(3, 5, 9, 11),
            low_by_vector=(0, 1),
            centre=(6, 9, 12, 14),
            var=16,
            inv=16,
            parts=17,
            spread=(20, 21, 22, 24),
            norm=(19, 21, 23, 23),
            norm_by_vector=(),
            feat=(21, 23, 25, 25),
            stack=(27, 30, 33, 39),
            logits=27, exp=28, gate=28, wb=31, const=35)
        AHEAD = Schedule(t=(0, 0, 0, 0), split=(1, 2, 3, 4), low_by_vector=(0, 1, 2, 3), centre=(2, 3, 4, 5), var=6, inv=7, parts=7,
                         spread=(8, 9, 10, 11), norm=(8, 9, 10, 11),
                         norm_by_vector=(0, 1, 2, 3), feat=(9, 10, 11, 12), stack=(12, 15, 35, 39),
                         logits=13, exp=13, gate=14, wb=15, const=33)
        LAST_AHEAD = 15
        AT_CONST = (2, 2, 8, 12)

        def groups_at(when, h):
            return [g for g in range(G) if when[g] == h]

        def x1_low(ops, eng, q, s, g):
            eng.wait_ge(ph_done, G * q + g + 1)
            ops.tensor_tensor(pl[:, g % 2, :], o[:, s, BG * g:BG * g + BG, :].rearrange("p b w -> p (b w)"),
                              ph[:, g % 2, :].bitcast(F32), ALU.subtract).then_inc(pl_done[g], 1)

        def body_of_chunks(eng, chunk):
            chunk(0, 0, 0, True, False)
            with eng.Fori(0, RP // 2 - 1) as j:
                chunk(2 * j + 1, 1, j, False, False)
                chunk(2 * j + 2, 0, j + 1, False, False)
            chunk(RP - 1, 1, RP // 2 - 1, False, True)

        def prep_half(prep, k, s, j, last, half):
            if not last:
                prep(STEADY, k + 1, 1 - s, j + s, half)
            prep(STEADY, k, s, j, half + HALVES)

        def body_of_images(eng, image, between=lambda: None):
            with eng.Fori(0, B // XRING - 1) as r:
                for i in range(XRING):
                    image(XRING * r + i, i, r, 0)
            between()
            for i in range(XRING):
                image(B - XRING + i, i, B // XRING - 1, XRING - 1 - i)

        with nc.Block() as block:

            @block.sync
            def _(sp):
                for s in stored[0] + stored[1]:
                    sp.sem_inc(s, 16)
                for h in range(2):
                    sp.dma_start(cwt[64 * h:64 * h + 64], cw).then_inc(s_cw, 16)
                    sp.dma_start(gb[64 * h:64 * h + 64, 0:1], gamma.rearrange("(c o) -> c o", o=1)).then_inc(s_cw, 16)

                def load_image(b, slot):
                    xb = x_pairs[b] if isinstance(b, int) else x_pairs[bass.ds(b, 1)].rearrange("o c k t w -> (o c) k t w")
                    sp.dma_start(xa[0:64, slot, 1:SLOTS, :], xb[:, :, 1, :]).then_inc(s_xa[slot], 16)
                    sp.dma_start(xa[64:128, slot, 0:RP, :], xb[:, :, 0, :]).then_inc(s_xa[slot], 16)

                sp.wait_ge(s_zero, 1)
                for b in range(XRING):
                    load_image(b, b)
                with sp.Fori(0, B // XRING - 1) as r:
                    for i in range(XRING):
                        sp.wait_ge(a_split, XRING * r + i + 1)
                        load_image(XRING * r + XRING + i, i)

                def load_chunk(q):
                    xq = x[:, :, bass.ds(2 * q, 2), :] if not isinstance(q, int) else x[:, :, 2 * q:2 * q + 2, :]
                    for h in range(2):
                        sp.dma_start(xin[64 * h:64 * h + 64], xq[:, :, h, :].rearrange("b c w -> c b w")).then_inc(x_loaded, 16)

                sp.wait_ge(a_split, B - XRING + XIN_OVER)
                load_chunk(0)
                sp.wait_ge(x1_done, G + RING2)
                load_chunk(1)

                def store(k, s, g):
                    images = slice(BG * g, BG * g + BG)
                    oq = out[images, :, bass.ds(2 * k, 2), :] if not isinstance(k, int) else out[images, :, 2 * k:2 * k + 2, :]
                    sp.wait_ge(out_done, G * k + g + 2)
                    for h in range(2):
                        sp.dma_start(oq[:, :, h, :].rearrange("b c w -> c b w"),
                                     o[64 * h:64 * h + 64, s, images]).then_inc(stored[s][g], 16)

                def chunk(k, s, loads):
                    store(k, s, 0)
                    if loads:
                        sp.wait_ge(x1_done, G * k + 2 * G + RING2)
                        load_chunk(k + 2)
                    for g in range(1, G):
                        store(k, s, g)

                with sp.Fori(0, RP // 2 - 1) as j:
                    for s in range(2):
                        chunk(2 * j + s, s, True)
                chunk(RP - 2, 0, False)
                chunk(RP - 1, 1, False)
                for s in stored[0] + stored[1]:
                    sp.wait_ge(s, 32 * (RP // 2) + 16)

            @block.gpsimd
            def _(pool):
                for s, n in ((x1_done, RING2), *((u, 1) for u in u_done)):
                    pool.sem_inc(s, n)
                nc.gpsimd.memset(ident[:], 0.0).then_inc(s_const, 1)
                nc.gpsimd.memset(halves[:], 0.0).then_inc(s_const, 1)
                nc.gpsimd.memset(ones64[:], 0.0)
                nc.gpsimd.memset(var_ones[:], 0.0)
                nc.gpsimd.memset(low_pattern[:], 0.0)
                nc.gpsimd.memset(tmp[:, 0:P], 0.0).then_inc(s_const, 1)
                pool.wait_ge(s_const, 3)
                nc.gpsimd.affine_select(out=ident[:], in_=ident[:], compare_op=ALU.not_equal, fill=1.0, base=0,
                                        pattern=[[-1, P]], channel_multiplier=1).then_inc(s_const, 1)
                for n, base in enumerate((0, C, -C)):
                    pool.wait_ge(s_const, 4 + n)
                    nc.gpsimd.affine_select(out=halves[:], in_=halves[:], compare_op=ALU.not_equal, fill=0.5, base=base,
                                            pattern=[[-1, P]], channel_multiplier=1).then_inc(s_const, 1)
                for h in range(2):
                    pool.wait_ge(s_const, 7 + h)
                    nc.gpsimd.memset(ones64[64 * h:64 * h + 64, 64 * h:64 * h + 64], 1.0 / C).then_inc(s_const, 1)
                for h in range(2):
                    pool.wait_ge(s_const, 9 + h)
                    nc.gpsimd.memset(var_ones[64 * h:64 * h + 64, h:h + 3:2], 1.0 / C).then_inc(s_const, 1)
                pool.wait_ge(s_const, 11)
                nc.gpsimd.affine_select(out=low_pattern[:], in_=low_pattern[:], compare_op=ALU.not_equal, fill=-1.0, base=-2,
                                        pattern=[[-32, G], [-1, 2]], channel_multiplier=1).then_inc(s_const, 1)
                for n in range(2 * G):
                    pool.wait_ge(s_const, 12 + n)
                    nc.gpsimd.affine_select(out=tmp[:, 0:P].rearrange("p (h m) -> p h m", h=2), in_=tmp[:, 0:P].rearrange("p (h m) -> p h m", h=2),
                                            compare_op=ALU.not_equal, fill=-0.5, base=-32 * (n // 2) - 2 * (n % 2),
                                            pattern=[[-1, 2], [0, C]], channel_multiplier=1).then_inc(s_const, 1)

                dma = pool.dma_start
                for i, vec in enumerate((g1, v1, b1, m1, be1, g2, v2)):
                    dma(rows[:, i, :], vec.rearrange("(o e) h -> o (e h)", o=1).broadcast_to([P, E * C])).then_inc(s_ffn, 16)
                for i, vec in enumerate((g2, v2, b2, m2, be2)):
                    dma(cols[:, i, :], vec.rearrange("(q two) h -> (two h) q", two=2), allow_slow_non_contiguous=True).then_inc(s_ffn, 16)
                for h in range(2):
                    dma(wraw[64 * h:64 * h + 64], W1.rearrange("e d h -> d e h")).then_inc(s_ffn, 16)
                dma(wo[:], Wo.rearrange("(q two) h d -> (two h) q d", two=2)).then_inc(s_ffn, 16)
                dma(gb[0:64, 1:2], beta.rearrange("(c o) -> c o", o=1)).then_inc(s_ffn, 16)
                dma(gb[64:128, 1:2], beta.rearrange("(c o) -> c o", o=1)).then_inc(s_ffn, 16)
                for h in range(2):
                    dma(brb[:, h, :], br.rearrange("(o e) -> o e", o=1).broadcast_to([W, E])).then_inc(s_ffn, 16)
                pool.wait_ge(s_zero, 2)
                for h in range(2):
                    dma(wr[64 * h:64 * h + 64, h, :], Wr).then_inc(s_ffn, 16)
                    dma(expert_const[E * h:E * h + E, 64 * h:64 * h + 64], bo).then_inc(s_w2, 16)
                    w2h = W2.rearrange("(q two) h k -> two h q k", two=2)[h]
                    dma(w2raw[64 * h:64 * h + 64, :, 64 * h:64 * h + 64], w2h).then_inc(s_w2, 16)

                T = nc.gpsimd
                count = [0]

                def step(ins):
                    count[0] += 1
                    ins.then_inc(f_pool, 1)
                    pool.wait_ge(f_pool, count[0])

                def inverse_root(var, first):
                    step(T.tensor_tensor(var, var, first, ALU.mult))
                    step(T.tensor_tensor(var, var, first, ALU.mult))
                    step(T.tensor_scalar(var, var, -0.5, 1.5, ALU.mult, ALU.add))
                    step(T.tensor_tensor(first, first, var, ALU.mult))

                r1 = lambda i: rows[:, i, :]
                c1 = lambda i: cols[:, i, :]
                pool.wait_ge(s_ffn, 16 * N_FFN)
                pool.wait_ge(s_dve, DVE_SPREAD)
                step(T.tensor_scalar(r1(1), r1(1), BNF_EPS, None, ALU.add))
                step(T.tensor_scalar(r1(6), r1(6), BNF_EPS, None, ALU.add))
                step(T.tensor_scalar(c1(1), c1(1), BNF_EPS, None, ALU.add))
                step(T.tensor_tensor(r1(2), r1(2), r1(3), ALU.subtract))
                step(T.tensor_tensor(c1(2), c1(2), c1(3), ALU.subtract))
                step(T.tensor_scalar(wr[:], wr[:], 1.0 / B, None, ALU.mult))
                pool.wait_ge(f_act, 6)
                inverse_root(r1(1), r1(3))
                inverse_root(c1(1), c1(5))
                inverse_root(r1(6), tmp[:])
                step(T.tensor_tensor(r1(6), tmp[:], r1(5), ALU.mult))
                step(T.tensor_tensor(c1(1), c1(5), c1(0), ALU.mult))
                step(T.tensor_tensor(r1(1), r1(3), r1(0), ALU.mult))
                step(T.tensor_tensor(r1(2), r1(2), r1(1), ALU.mult))
                step(T.tensor_tensor(tmp[:], wraw[:].rearrange("p e h -> p (e h)"), r1(1), ALU.mult))
                step(T.tensor_tensor(r1(2), r1(2), r1(4), ALU.add))
                step(T.tensor_tensor(c1(2), c1(2), c1(1), ALU.mult))
                step(T.tensor_tensor(bias2[:], c1(2), c1(4), ALU.add))
                step(T.tensor_scalar(negb2[:], bias2[:], -1.0, None, ALU.mult))
                for q in range(PAIRS):
                    for h in range(2):
                        half = slice(64 * h, 64 * h + 64)
                        step(T.tensor_copy(c2sel[half, q, 2 * q + h:2 * q + h + 1], bias2[half, q:q + 1]))
                w2f = w2raw[:].rearrange("p q m -> p (q m)")
                pool.wait_ge(s_w2, 16 * N_W2)
                step(T.tensor_tensor(w2f, w2f, r1(6), ALU.mult))

                def x1(q, s, j, g):
                    if g == 0:
                        pool.wait_ge(x_loaded, 32 * q + 32)
                    pool.wait_ge(stored[s][g], 32 * j + 16)
                    pool.wait_ge(clip_done, G * q + g + 1)
                    og = o[:, s, BG * g:BG * g + BG, :]
                    nc.gpsimd.tensor_tensor(og, xin[:, BG * g:BG * g + BG, :],
                                            t[:, g].rearrange("p (b w) -> p b w", w=W), ALU.add).then_inc(x1_done, 1)

                def norm(q, g):
                    pool.wait_ge(rb_done[g], q + 1)
                    nc.gpsimd.tensor_tensor(xc[:, g], xc[:, g], t[:, g], ALU.mult).then_inc(u_done[g], 1)

                def add_const(k, s, g):
                    if g == 0:
                        pool.wait_ge(g_done, k + 2)
                    og = o[:, s, BG * g:BG * g + BG, :]
                    nc.gpsimd.tensor_tensor(og, og, gconst[:, s:s + 1, :].broadcast_to([P, BG, W]), ALU.add).then_inc(x1g_done, 1)

                def prep(at, q, s, j, h):
                    for g in groups_at(at.split, h):
                        if g not in at.low_by_vector:
                            x1_low(nc.gpsimd, pool, q, s, g)
                    for g in groups_at(at.t, h):
                        x1(q, s, j, g)
                    for g in groups_at(at.norm, h):
                        if g not in at.norm_by_vector:
                            norm(q, g)

                def chunk(k, s, j, first, last):
                    for n in range(UNITS):
                        unit = UNITS * k + n
                        prep_half(prep, k, s, j, last, 2 * n)
                        if n == 0:
                            pool.wait_ge(wb_done, k + 1)
                        pool.wait_ge(relu1_done, unit + 2)
                        nc.gpsimd.tensor_tensor(v[:, n % 2, 1].rearrange("p (b w) -> p b w", w=W),
                                                v[:, n % 2, 1].rearrange("p (b w) -> p b w", w=W),
                                                wb[:, s, n % PAIRS, 1:2, :].broadcast_to([P, BG, W]),
                                                ALU.mult).then_inc(v1_done, 1)
                        for g in groups_at(AT_CONST, n):
                            add_const(k, s, g)
                        prep_half(prep, k, s, j, last, 2 * n + 1)

                for h in range(LAST_AHEAD + 1):
                    prep(AHEAD, 0, 0, 0, h)
                body_of_chunks(pool, chunk)

            @block.tensor
            def _(pe):
                for s, n in ((a_conv, RINGS), (centre_done, RING2), (z2_full[0], RING2), (z2_full[1], RING2), (l3_done, RING2)):
                    pe.sem_inc(s, n)
                mm = nc.tensor.matmul

                pe.wait_ge(s_act, 2)
                for kx in range(3):
                    for n, first in enumerate((1, 0, 3, 2)):
                        at = ps[:, kx // 2, 256 * (kx % 2) + 64 * n:256 * (kx % 2) + 64 * n + 64]
                        last = mm(at, cwsign[:, kx, first:first + 2, :].rearrange("p a c -> p (a c)"), identb[:], start=True, stop=True)
                last.then_inc(s_pe, 1)
                def centre_image(b, i):
                    pe.wait_ge(a_split, b + 1)
                    for g in range(GA):
                        lo, hi = slot_group(g)
                        pe.wait_ge(a_signed, GA * b + g + 1)
                        at = ps[:, g, 0:(hi - lo) * W]
                        mm(at, centre[:], xhi[:, i % 2, lo:hi, :], start=True, stop=False)
                        mm(at, centre[:], xlo[:, i % 2, lo:hi, :], start=False, stop=True).then_inc(a_centred, 1)

                def conv_image(b, i):
                    for g in range(GA):
                        pe.wait_ge(a_signed, GA * b + g + 1 + RINGA)
                        pe.wait_ge(a_kept, GA * b + g + 1)
                        at = ps[:, GA + g, 0:KG * W]
                        for kx in range(3):
                            for nxt in range(2):
                                last = mm(at, convw[:, kx, nxt, :], sgn[:, i % 2, KG * g + nxt:KG * g + nxt + KG, kx:kx + W],
                                          start=(kx + nxt == 0), stop=(kx + nxt == 3))
                        last.then_inc(a_conv, 1)

                pe.wait_ge(s_act, 3)
                centre_image(0, 0)

                def image(b, i, r, left):
                    if not isinstance(b, int) or left:
                        centre_image(b + 1, i + 1)
                    conv_image(b, i)

                body_of_images(pe, image)

                for n in range(2):
                    pe.wait_ge(a_stats, B + 1 + 3 * n)
                    mm(ps[:, 0, n:n + 1], halves[:], bn[:, 4 + n:5 + n], start=True, stop=True).then_inc(s_pe, 1)

                pe.wait_ge(f_pool, FOLD_TMP)
                mm(ps[:, 2], ones64[:], tmp[:], start=True, stop=True).then_inc(s_pe, 1)

                def layer1(k, n):
                    unit, g, q = UNITS * k + n, n // PAIRS, n % PAIRS
                    if q == 0:
                        pe.wait_ge(slo_done, G * k + g + 1 + G)
                    for par in range(2):
                        pe.wait_ge(hlo_done[par], unit + 1)
                        at = ps[:, 2 * (n % 2) + par, 0:NG]
                        mm(at, w1hi[:, P * q:P * q + P], stack[:, par, g, :], start=True, stop=False)
                        mm(at, w1lo[:, P * q:P * q + P], stack[:, par, g, :], start=False, stop=True).then_inc(z1_full[par], 1)

                def layer2(k, n):
                    unit, q = UNITS * k + n, n % PAIRS
                    for par in range(2):
                        pe.wait_ge(hhi_done[par], unit + 1)
                        pe.wait_ge((v0_done, relu1_done)[par], unit + 1)
                        at = ps[:, 4 + par, 0:NG]
                        mm(at, w2hi[:, q, :], hhi[:, n % 2, par, :], start=True, stop=False)
                        mm(at, w2lo[:, q, :], hhi[:, n % 2, par, :], start=False, stop=False)
                        pe.wait_ge(hlo_done[par], unit + 1 + RING2)
                        mm(at, w2hi[:, q, :], hlo[:, n % 2, par, :], start=False, stop=True).then_inc(z2_full[par], 1)

                def layer3(k, n):
                    unit, g, q = UNITS * k + n, n // PAIRS, n % PAIRS
                    pe.wait_ge(v0_done, unit + 2)
                    pe.wait_ge(v1_done, unit + 1)
                    if q == 0:
                        pe.wait_ge(out_done, G * k + g + 1)
                    for par in range(2):
                        last = mm(ps[64 * par:64 * par + 64, 6, 0:NG], wo[:, q, :], v[:, n % 2, par, :],
                                  start=(q == 0), stop=(q == PAIRS - 1))
                    last.then_inc(l3_done, 1)

                def prep(at, q, s, j, h):
                    for g in groups_at(at.centre, h):
                        pe.wait_ge(pl_done[g], q + 1)
                        pe.wait_ge(xc_done, G * q + g + 1)
                        if g == 0:
                            pe.wait_ge(g_done, q + 1)
                        mm(misc[:, 0:NG], centre[:], ph[:, g % 2, :], start=True, stop=False)
                        mm(misc[:, 0:NG], centre[:], pl[:, g % 2, :], start=False, stop=True).then_inc(centre_done, 1)
                    if h == at.var:
                        pe.wait_ge(xc_done, G * q + G + 1)
                        for g in range(G):
                            last = mm(misc[32 * g:32 * g + 32, 0:NG], var_ones[:], t[:, g, :], start=True, stop=True)
                        last.then_inc(var_done, 1)
                    for g in groups_at(at.spread, h):
                        if g == 0:
                            pe.wait_ge(rs_done, q + 1)
                        elif g - 1 in at.norm_by_vector:
                            pe.wait_ge(u_done[g - 1], q + 2)
                        else:
                            pe.wait_ge(rb_done[g - 1], q + 1)
                        r = slice(32 * g, 32 * g + 32)
                        mm(misc[:, 0:NG], spread[r, :], rparts[r, :], start=True, stop=True).then_inc(rb_full, 1)
                    if h == at.logits:
                        pe.wait_ge(feat_done, q + 1)
                        if G - 1 in at.norm_by_vector:
                            pe.wait_ge(u_done[G - 1], q + 2)
                        else:
                            pe.wait_ge(rb_done[G - 1], q + 1)
                        mm(misc[0:W, 0:2 * E], feat[:], wr[:].rearrange("p a e -> p (a e)"), start=True, stop=True).then_inc(logits_done, 1)
                    if h == at.wb:
                        pe.wait_ge(gate_done, q + 1)
                        for pair in range(PAIRS):
                            for par in range(2):
                                col = (2 * pair + par) * W
                                for half in range(2):
                                    e = 2 * pair + half
                                    mm(misc[64 * half:64 * half + 64, col:col + W], gate_w[:, par, e:e + 1].broadcast_to([P, C]),
                                       ident[:, 0:W], start=True, stop=True)
                        mm(misc[0:2 * E, NG:NG + W], gate_w[:].rearrange("p a e -> p (a e)"), ident[:, 0:W],
                           start=True, stop=True).then_inc(wb_full, 1)
                    if h == at.const:
                        pe.wait_ge(wb_done, q + 1)
                        mm(misc[:, 0:W], expert_const[:], wT[:], start=True, stop=True).then_inc(g_full, 1)

                def chunk(k, s, j, first, last):
                    for n in range(UNITS):
                        if n + 1 < UNITS:
                            layer1(k, n + 1)
                        elif not last:
                            layer1(k + 1, 0)
                        prep_half(prep, k, s, j, last, 2 * n)
                        layer2(k, n)
                        prep_half(prep, k, s, j, last, 2 * n + 1)
                        if n:
                            layer3(k, n - 1)
                        elif not first:
                            layer3(k - 1, UNITS - 1)
                    if last:
                        layer3(k, UNITS - 1)

                for h in range(AHEAD.logits):
                    prep(AHEAD, 0, 0, 0, h)
                pe.wait_ge(f_pool, FOLD_ALL)
                for q in range(PAIRS):
                    last = mm(ps[0:2 * E, 3, 0:C], c2sel[:, q, :], wo[:, q, :], start=(q == 0), stop=(q == PAIRS - 1))
                last.then_inc(s_pe, 1)
                pe.wait_ge(f_dve, FOLD_DVE)
                for h in range(AHEAD.logits, LAST_AHEAD + 1):
                    if h == AHEAD.wb:
                        layer1(0, 0)
                    prep(AHEAD, 0, 0, 0, h)
                body_of_chunks(pe, chunk)

            @block.scalar
            def _(act):
                for s, n in ((a_signed, RINGA), (a_kept, RINGA), (relu1_done, 1), (xc_done, 1), (g_done, 1)):
                    act.sem_inc(s, n)
                for g in AHEAD.norm_by_vector:
                    act.sem_inc(rb_done[g], 1)
                A = nc.scalar.activation
                act.wait_ge(s_dve, 6)
                A(bn[:, 8:9], bn[:, 7:8], ACT.Sqrt, scale=1.0 / (C * TAPS - 1)).then_inc(s_act, 1)
                A(cwsign[:, :, 1:4, :], cwt[0:64].rearrange("p ci ky kx -> p kx ky ci"), ACT.Sign).then_inc(s_act, 1)
                act.preload_act_table_set("natural_log_exp_and_others")
                act.wait_ge(s_pe, 1)
                A(convw[:, 0:2].rearrange("p k a m -> p (k a m)"), ps[:, 0, :], ACT.Copy)
                A(convw[:, 2].rearrange("p a m -> p (a m)"), ps[:, 1, 0:256], ACT.Copy).then_inc(s_act, 1)
                def sign_image(b, i):
                    act.wait_ge(a_conv, GA * b + GA)
                    for g in range(GA):
                        lo, hi = slot_group(g)
                        act.wait_ge(a_centred, GA * b + g + 1)
                        A(sgn[:, i % 2, lo:hi, 1:W + 1], ps[:, g, 0:(hi - lo) * W].rearrange("p (k w) -> p k w", w=W),
                          ACT.Sign).then_inc(a_signed, 1)

                def keep_image(b):
                    for g in range(GA):
                        act.wait_ge(a_conv, GA * b + g + 1 + RINGS)
                        yb = y[:, KG * g:KG * g + KG, b, :] if isinstance(b, int) else \
                            y[:, KG * g:KG * g + KG, bass.ds(b, 1), :].rearrange("p k o w -> p (k o) w")
                        A(yb, ps[:, GA + g, 0:KG * W].rearrange("p (k w) -> p k w", w=W), ACT.Copy).then_inc(a_kept, 1)

                act.wait_ge(s_zero, 2)
                sign_image(0, 0)

                def image(b, i, r, left):
                    if not isinstance(b, int) or left:
                        sign_image(b + 1, i + 1)
                    keep_image(b)

                def fold_roots():
                    act.wait_ge(f_pool, FOLD_VAR)
                    count = 0
                    for var, first in ((rows[:, 1, :], rows[:, 3, :]), (cols[:, 1, :], cols[:, 5, :]), (rows[:, 6, :], tmp[:])):
                        A(first, var, ACT.Ln).then_inc(f_act, 1)
                        act.wait_ge(f_act, count + 1)
                        A(first, first, ACT.Exp, scale=-0.5).then_inc(f_act, 1)
                        count += 2

                body_of_images(act, image, fold_roots)
                act.preload_act_table_set("sqrt_and_others")
                act.wait_ge(a_stats, B + 5)
                A(bn[:, 11:12], bn[:, 10:11], ACT.Sqrt).then_inc(s_act, 1)
                act.preload_act_table_set("natural_log_exp_and_others")

                def relu_hi(k, n):
                    unit = UNITS * k + n
                    for par in range(2):
                        act.wait_ge(z1_full[par], unit + 1)
                        act.wait_ge(z2_full[par], unit + 1)
                        A(hhi[:, n % 2, par, :], ps[:, 2 * (n % 2) + par, 0:NG], ACT.Relu).then_inc(hhi_done[par], 1)

                def relu1(k, n):
                    unit = UNITS * k + n
                    act.wait_ge(z2_full[1], unit + 1 + RING2)
                    act.wait_ge(l3_done, unit + 1)
                    A(v[:, n % 2, 1, :], ps[:, 5, 0:NG], ACT.Relu, bias=bias2[:, n % PAIRS:n % PAIRS + 1]).then_inc(relu1_done, 1)

                def prep(at, q, s, j, h):
                    for g in groups_at(at.split, h):
                        act.wait_ge(x1_done, G * q + g + 1 + RING2)
                        act.wait_ge(centre_done, G * q + g + 1)
                        A(ph[:, g % 2, :], o[:, s, BG * g:BG * g + BG, :].rearrange("p b w -> p (b w)"), ACT.Copy).then_inc(ph_done, 1)
                    for g in groups_at(at.centre, h):
                        act.wait_ge(centre_done, G * q + g + 1 + RING2)
                        act.wait_ge(slo_done, G * q + g + 1)
                        A(t[:, g], misc[:, 0:NG], ACT.Square)
                        A(xc[:, g, :], misc[:, 0:NG], ACT.Copy).then_inc(xc_done, 1)
                    for g in groups_at(at.t, h):
                        act.wait_ge(u_done[g], q + 1)
                        yq = y[:, q, BG * g:BG * g + BG, :] if isinstance(q, int) else \
                            y[:, bass.ds(q, 1), BG * g:BG * g + BG, :].rearrange("p o b w -> p (o b) w")
                        A(t[:, g].rearrange("p (b w) -> p b w", w=W), yq, ACT.Identity, bias=OFFSET, scale=SCALE).then_inc(t_done, 1)
                    if h == at.var:
                        act.wait_ge(var_done, q + 1)
                        A(rs[:], misc[:, 0:NG], ACT.Ln, bias=LN_EPS).then_inc(root_steps, 1)
                        act.wait_ge(root_steps, 2 * q + 1)
                        A(rs[:], rs[:], ACT.Exp, scale=-0.5).then_inc(root_steps, 1)
                        act.wait_ge(root_steps, 2 * q + 2)
                        A(sq[:], rs[:], ACT.Square).then_inc(root_done, 1)
                    for g in groups_at(at.spread, h):
                        if g not in at.norm_by_vector:
                            act.wait_ge(rb_full, G * q + g + 1)
                            A(t[:, g], misc[:, 0:NG], ACT.Copy).then_inc(rb_done[g], 1)
                    for g in groups_at(at.stack, h):
                        act.wait_ge(u_done[g], q + 2)
                        for par in range(2):
                            half = slice(64 * par, 64 * par + 64)
                            A(stack[half, par, g, :], xc[half, g, :], ACT.Copy, bias=SHIFT).then_inc(shi_done, 1)
                    if h == at.exp:
                        act.wait_ge(gate_sub, q + 1)
                        A(gate_e[:], gate[:], ACT.Exp).then_inc(gate_exp, 1)
                    if h == at.wb:
                        act.wait_ge(wb_full, q + 1)
                        A(wT[:], misc[0:2 * E, NG:NG + W], ACT.Copy)
                        A(wb[:, s].rearrange("p a b w -> p (a b w)"), misc[:, 0:NG], ACT.Copy).then_inc(wb_done, 1)
                    if h == at.const:
                        act.wait_ge(g_full, q + 1)
                        A(gconst[:, s, :], misc[:, 0:W], ACT.Copy).then_inc(g_done, 1)

                def chunk(k, s, j, first, last):
                    for n in range(UNITS):
                        if n + 1 < UNITS:
                            relu_hi(k, n + 1)
                        elif not last:
                            relu_hi(k + 1, 0)
                        prep_half(prep, k, s, j, last, 2 * n)
                        relu1(k, n)
                        prep_half(prep, k, s, j, last, 2 * n + 1)

                act.wait_ge(s_bn, 1)
                for h in range(LAST_AHEAD + 1):
                    prep(AHEAD, 0, 0, 0, h)
                relu_hi(0, 0)
                body_of_chunks(act, chunk)

            @block.vector
            def _(dve):
                V = nc.vector
                for s, n in ((slo_done, G), (hlo_done[0], RING2), (hlo_done[1], RING2), (v0_done, 1), (out_done, 1)):
                    dve.sem_inc(s, n)
                V.memset(xa[:, :, 0:1, :], 0.0)
                V.memset(xa[:, :, RP:SLOTS, :], 0.0).then_inc(s_zero, 1)
                V.memset(sgn[:], 0.0)
                V.memset(w2raw[:], 0.0)
                V.memset(wr[:], 0.0)
                V.memset(expert_const[:], 0.0)
                V.memset(c2sel[:], 0.0)
                V.memset(cwsign[:], 0.0).then_inc(s_zero, 1)

                count = [0]

                def step(ins):
                    count[0] += 1
                    ins.then_inc(s_dve, 1)
                    dve.wait_ge(s_dve, count[0])

                dve.wait_ge(s_cw, 16 * N_CW)
                dve.wait_ge(s_zero, 2)
                cflat = cwt[:].rearrange("p a b c -> p (a b c)")
                step(V.tensor_reduce(bn[:, 3:4], cflat, AX.X, ALU.add))
                step(V.tensor_scalar(bn[:, 3:4], bn[:, 3:4], 1.0 / (C * TAPS), None, ALU.mult))
                step(V.tensor_scalar(cflat, cflat, bn[:, 3:4], None, ALU.subtract))
                step(V.tensor_tensor(cwa[:], cflat, cflat, ALU.mult))
                step(V.tensor_reduce(bn[:, 7:8], cwa[:], AX.X, ALU.add))
                dve.wait_ge(s_const, 9)
                step(V.tensor_copy(identb[:], ident[0:64, 0:64]))
                V.tensor_tensor(centre[:], ident[:], ones64[:], ALU.subtract)

                def fold_parts():
                    def then(ins):
                        folded[0] += 1
                        ins.then_inc(f_dve, 1)
                        dve.wait_ge(f_dve, folded[0])

                    folded = [0]
                    row, w2f, w2h, w2l = rows[:, 2, :], *(a[:].rearrange("p q m -> p (q m)") for a in (w2raw, w2hi, w2lo))
                    dve.wait_ge(f_pool, FOLD_ALL)
                    dve.wait_ge(s_pe, 4)
                    then(V.scalar_tensor_tensor(out=row, in0=row, scalar=1.0 / (C * SHIFT), in1=ps[:, 2],
                                                op0=ALU.mult, op1=ALU.subtract))
                    then(V.tensor_tensor(tmp[:], tmp[:], row, ALU.add))
                    then(V.tensor_copy(w1hi[:], tmp[:]))
                    then(V.tensor_tensor(w1lo[:], tmp[:], w1hi[:].bitcast(F32), ALU.subtract))
                    then(V.tensor_copy(w2h, w2f))
                    then(V.tensor_tensor(w2l, w2f, w2h.bitcast(F32), ALU.subtract))

                def split(b, i, r):
                    s4 = i % XRING
                    dve.wait_ge(s_xa[s4], 32 * (r + i // XRING) + 32)
                    if not (isinstance(b, int) and b < 2):
                        dve.wait_ge(a_centred, GA * b - GA)
                    V.tensor_copy(xhi[:, i % 2], xa[:, s4]).then_inc(a_hi, 1)
                    dve.wait_ge(a_hi, b + 1)
                    V.tensor_tensor(xlo[:, i % 2], xa[:, s4], xhi[:, i % 2].bitcast(F32), ALU.subtract).then_inc(a_split, 1)

                def image_stats(b):
                    for g in range(GA):
                        dve.wait_ge(a_kept, GA * b + g + 1 + RINGA)
                        k = slice(KG * g, KG * g + KG)
                        if isinstance(b, int):
                            yb, sb_ = y[:, k, b, :], stats[:, b, g, :]
                        else:
                            yb = y[:, k, bass.ds(b, 1), :].rearrange("p k o w -> p (k o) w")
                            sb_ = stats[:, bass.ds(b, 1), g, :].rearrange("p o s -> p (o s)")
                        last = V.bn_stats(sb_, yb)
                    last.then_inc(a_stats, 1)

                split(0, 0, 0)
                split(1, 1, 0)

                step(V.scalar_tensor_tensor(out=cwa[:], in0=cflat, scalar=-1.0, in1=cflat, op0=ALU.mult, op1=ALU.max))
                step(V.tensor_reduce(bn[:, 9:10], cwa[:], AX.X, ALU.add))

                dve.wait_ge(s_act, 1)
                step(V.reciprocal(SW, bn[:, 8:9]))
                step(V.tensor_scalar(bn[:, 9:10], bn[:, 9:10], SW, SQRT2 / (C * TAPS), ALU.mult, ALU.mult))
                step(V.tensor_scalar(SW.bitcast(I32), bn[:, 9:10].bitcast(I32), EXP_MASK, None, ALU.bitwise_and))

                dve.wait_ge(s_const, 20)
                V.tensor_reduce(low_rows[:], low_pattern[:].rearrange("p g i -> p (g i)"), AX.X, ALU.add)
                step(V.tensor_copy(spread[:], tmp[:, 0:P]))


                def image(b, i, r, left):
                    if not isinstance(b, int) or left >= 2:
                        split(b + 2, i + 2, r)
                    image_stats(b)

                body_of_images(dve, image)

                mean, var = bn[:, 12:13], bn[:, 13:14]
                dve.wait_ge(a_stats, B)
                V.bn_aggr(bn[:, 4:6], stats[:].rearrange("p b g s -> p (b g s)")).then_inc(a_stats, 1)
                dve.wait_ge(s_pe, 2)
                V.tensor_copy(mean, ps[:, 0, 0:1]).then_inc(a_stats, 1)
                dve.wait_ge(a_stats, B + 2)
                V.tensor_tensor(bn[:, 14:15], bn[:, 4:5], mean, ALU.subtract).then_inc(a_stats, 1)
                dve.wait_ge(a_stats, B + 3)
                V.scalar_tensor_tensor(out=bn[:, 5:6], in0=bn[:, 14:15], scalar=bn[:, 14:15], in1=bn[:, 5:6],
                                       op0=ALU.mult, op1=ALU.add).then_inc(a_stats, 1)
                dve.wait_ge(s_pe, 3)
                V.tensor_scalar(bn[:, 13:14], ps[:, 0, 1:2], SW, None, ALU.mult).then_inc(d_bn, 1)
                dve.wait_ge(d_bn, 1)
                V.tensor_scalar(bn[:, 10:11], var, SW, BN1_EPS, ALU.mult, ALU.add).then_inc(a_stats, 1)
                dve.wait_ge(s_act, 4)
                V.reciprocal(bn[:, 15:16], bn[:, 11:12]).then_inc(d_bn, 1)
                dve.wait_ge(d_bn, 2)
                V.tensor_scalar(bn[:, 14:15], bn[:, 15:16], SW, None, ALU.mult).then_inc(d_bn, 1)
                dve.wait_ge(d_bn, 3)
                V.tensor_scalar(SCALE, bn[:, 14:15], gb[:, 0:1], None, ALU.mult).then_inc(d_bn, 1)
                dve.wait_ge(d_bn, 4)
                V.tensor_scalar(bn[:, 14:15], mean, SCALE, None, ALU.mult).then_inc(d_bn, 1)
                dve.wait_ge(d_bn, 5)
                V.tensor_tensor(OFFSET, gb[:, 1:2], bn[:, 14:15], ALU.subtract).then_inc(s_bn, 1)

                def relu_lo(k, n, par):
                    dve.wait_ge(hhi_done[par], UNITS * k + n + 1)
                    V.scalar_tensor_tensor(out=hlo[:, n % 2, par, :], in0=ps[:, 2 * (n % 2) + par, 0:NG], scalar=0.0,
                                           in1=hhi[:, n % 2, par, :].bitcast(F32), op0=ALU.max, op1=ALU.subtract).then_inc(hlo_done[par], 1)

                def v0(k, s, n):
                    unit, q = UNITS * k + n, n % PAIRS
                    if n == 0:
                        dve.wait_ge(wb_done, k + 1)
                    dve.wait_ge(z2_full[0], unit + 1 + RING2)
                    dve.wait_ge(l3_done, unit + 1)
                    V.scalar_tensor_tensor(out=v[:, n % 2, 0, :].rearrange("p (b w) -> p b w", w=W),
                                           in0=ps[:, 4, 0:NG].rearrange("p (b w) -> p b w", w=W), scalar=negb2[:, q:q + 1],
                                           in1=wb[:, s, q, 0:1, :].broadcast_to([P, BG, W]),
                                           op0=ALU.max, op1=ALU.mult).then_inc(v0_done, 1)

                def add_out(k, s, g):
                    dve.wait_ge(l3_done, UNITS * k + PAIRS * g + PAIRS + RING2)
                    dve.wait_ge(x1g_done, G * k + g + 1)
                    og = o[:, s, BG * g:BG * g + BG, :].rearrange("p b w -> p (b w)")
                    V.tensor_tensor(og, ps[:, 6, 0:NG], og, ALU.add).then_inc(out_done, 1)

                GATE_STEPS, RS_STEPS = 4, 3

                def prep(at, q, s, j, h):
                    for g in groups_at(at.t, h):
                        dve.wait_ge(t_done, G * q + g + 1)
                        V.tensor_scalar(t[:, g, :], t[:, g, :], 1.0, -1.0, ALU.min, ALU.max).then_inc(clip_done, 1)
                    for g in groups_at(at.split, h):
                        if g in at.low_by_vector:
                            x1_low(V, dve, q, s, g)
                    if h == at.inv:
                        dve.wait_ge(root_done, q + 1)
                        V.scalar_tensor_tensor(out=sq[:], in0=misc[:, 0:NG], scalar=LN_EPS, in1=sq[:],
                                               op0=ALU.add, op1=ALU.mult).then_inc(d_rs, 1)
                        dve.wait_ge(d_rs, RS_STEPS * q + 1)
                        V.scalar_tensor_tensor(out=rs[:], in0=sq[:], scalar=-3.0, in1=rs[:],
                                               op0=ALU.add, op1=ALU.mult).then_inc(d_rs, 1)
                    if h == at.parts:
                        dve.wait_ge(d_rs, RS_STEPS * q + 2)
                        V.tensor_copy(rhi[:], rs[:]).then_inc(d_rs, 1)
                        dve.wait_ge(d_rs, RS_STEPS * q + 3)
                        V.scalar_tensor_tensor(out=rparts[:], in0=rhi[:].bitcast(F32), scalar=low_rows[:], in1=rs[:],
                                               op0=ALU.mult, op1=ALU.add).then_inc(rs_done, 1)
                    for g in groups_at(at.spread, h):
                        if g in at.norm_by_vector:
                            dve.wait_ge(rb_full, G * q + g + 1)
                            V.tensor_tensor(xc[:, g], xc[:, g], misc[:, 0:NG], ALU.mult).then_inc(u_done[g], 1)
                    for g in groups_at(at.feat, h):
                        dve.wait_ge(u_done[g], q + 2)
                        V.tensor_reduce(feat4[:, g, :], xc[:, g, :].rearrange("p (b w) -> p w b", w=W), AX.X, ALU.add).then_inc(d_feat, 1)
                        if g == G - 1:
                            dve.wait_ge(d_feat, G * q + G)
                            V.tensor_reduce(feat[:], feat4[:].rearrange("p g w -> p w g"), AX.X, ALU.add).then_inc(feat_done, 1)
                    for g in groups_at(at.stack, h):
                        for par in range(2):
                            half = slice(64 * par, 64 * par + 64)
                            other = slice(64 - 64 * par, 128 - 64 * par)
                            dve.wait_ge(shi_done, 2 * (G * q + g) + par + 1)
                            last = V.scalar_tensor_tensor(out=stack[other, par, g, :], in0=xc[half, g, :], scalar=SHIFT,
                                                          in1=stack[half, par, g, :].bitcast(F32), op0=ALU.add, op1=ALU.subtract)
                        last.then_inc(slo_done, 1)
                    if h == at.logits:
                        dve.wait_ge(logits_done, q + 1)
                        V.tensor_tensor(gate[:].rearrange("p a e -> p (a e)"), misc[0:W, 0:2 * E], brb[:].rearrange("p a e -> p (a e)"), ALU.add).then_inc(d_gate, 1)
                        dve.wait_ge(d_gate, GATE_STEPS * q + 1)
                        V.tensor_reduce(gate_s[:, :, 0:1], gate[:], AX.X, ALU.max).then_inc(d_gate, 1)
                        dve.wait_ge(d_gate, GATE_STEPS * q + 2)
                        V.tensor_tensor(gate[:], gate[:], gate_s[:, :, 0:1].broadcast_to([W, 2, E]), ALU.subtract).then_inc(gate_sub, 1)
                    if h == at.gate:
                        dve.wait_ge(gate_exp, q + 1)
                        V.tensor_reduce(gate_s[:, :, 0:1], gate_e[:], AX.X, ALU.add).then_inc(d_gate, 1)
                        dve.wait_ge(d_gate, GATE_STEPS * q + 3)
                        V.reciprocal(gate_s[:, :, 1:2], gate_s[:, :, 0:1]).then_inc(d_gate, 1)
                        dve.wait_ge(d_gate, GATE_STEPS * q + 4)
                        V.tensor_tensor(gate_w[0:W], gate_e[:], gate_s[:, :, 1:2].broadcast_to([W, 2, E]), ALU.mult).then_inc(gate_done, 1)

                def chunk(k, s, j, first, last):
                    for n in range(UNITS):
                        ahead = (k, n + 1) if n + 1 < UNITS else (k + 1, 0)
                        if not (last and n + 1 == UNITS):
                            relu_lo(*ahead, 0)
                        v0(k, s, n)
                        if not (last and n + 1 == UNITS):
                            relu_lo(*ahead, 1)
                        if n == 0 and not first:
                            add_out(k - 1, 1 - s, G - 1)
                        elif n and n % PAIRS == 0:
                            add_out(k, s, n // PAIRS - 1)
                        prep_half(prep, k, s, j, last, 2 * n)
                        prep_half(prep, k, s, j, last, 2 * n + 1)
                    if last:
                        add_out(k, s, G - 1)

                V.memset(gate_w[:], 0.0).then_inc(d_bn, 1)
                dve.wait_ge(d_bn, 6)
                for h in range(AHEAD.logits):
                    if h == AHEAD.var:
                        fold_parts()
                    prep(AHEAD, 0, 0, 0, h)
                dve.wait_ge(s_pe, 5)
                V.tensor_tensor(expert_const[:, 0:C], expert_const[:, 0:C], ps[0:2 * E, 3, 0:C], ALU.add).then_inc(f_dve, 1)
                for h in range(AHEAD.logits, LAST_AHEAD + 1):
                    prep(AHEAD, 0, 0, 0, h)
                for par in range(2):
                    relu_lo(0, 0, par)
                body_of_chunks(dve, chunk)


_INS = ["x", "L0_conv_weight", "L0_conv_gamma", "L0_conv_beta", "L0_ffn_Wr", "L0_ffn_br", "L0_ffn_W1", "L0_ffn_b1",
        "L0_ffn_g1", "L0_ffn_be1", "L0_ffn_m1", "L0_ffn_v1", "L0_ffn_W2", "L0_ffn_b2", "L0_ffn_g2", "L0_ffn_be2",
        "L0_ffn_m2", "L0_ffn_v2", "L0_ffn_Wo", "L0_ffn_bo"]


def kernel(**inputs):
    import numpy as _np
    import concourse.bacc as _bacc
    from concourse.bass_utils import run_bass_kernel_spmd as _run

    nc = _bacc.Bacc("TRN2", target_bir_lowering=False, num_devices=1)
    arrays, args = {}, []
    for name in _INS:
        a = _np.ascontiguousarray(inputs[name])
        arrays[f"in_{name}"] = a
        args.append(nc.dram_tensor(f"in_{name}", a.shape, mybir.dt.from_np(a.dtype), kind="ExternalInput").ap())
    args.append(nc.dram_tensor("out", (B, C, H, W), F32, kind="ExternalOutput").ap())
    metaformer_kernel(nc, *args)
    r = _run(nc, [arrays], core_ids=[0])
    return r.results[0]["out"]
```
